# Optimizing a Trainium2 kernel written in Bass

```python
import numpy as np
import jax
import jax.numpy as jnp

def _softmax(x, axis=-1):
    return jax.nn.softmax(x, axis=axis)

def _gelu(x):
    return jax.nn.gelu(x, approximate=True)

def _silu(x):
    return jax.nn.silu(x)

def _sigmoid(x):
    return jax.nn.sigmoid(x)

def _layernorm(x, axis=-1, eps=1e-05):
    m = jnp.mean(x, axis=axis, keepdims=True)
    v = jnp.var(x, axis=axis, keepdims=True)
    return (x - m) / jnp.sqrt(v + eps)

def _scatter_add(tgt, idx, src, axis=0):
    return tgt.at[idx].add(src)

def _segment_sum(src, seg, n):
    return jax.ops.segment_sum(src, seg, n)
kernel_name = 'mk_adaln_d1_jaxref_r4_ca555a'

def setup_inputs(seed: int=0):
    np.random.seed(seed)
    _w = jnp.asarray

    def _L0_attn_setup():
        import jax, jax.numpy as jnp
        import numpy as np
        B, T, D, R = (8, 512, 512, 4)
        key = jax.random.key(seed)
        ks = jax.random.split(key, 9)
        u = jax.random.normal(ks[0], (B, T, D), dtype=jnp.float32)
        a = 3.0 + 0.2 * jax.random.uniform(ks[1], (D,), dtype=jnp.float32)
        b = 0.02 * jax.random.normal(ks[2], (D,), dtype=jnp.float32)
        c = 0.02 * jax.random.normal(ks[3], (D,), dtype=jnp.float32)
        d = 0.02 * jax.random.normal(ks[4], (D,), dtype=jnp.float32)
        gate_w = jax.random.normal(ks[5], (D, D), dtype=jnp.float32) / np.float32(np.sqrt(D))
        gate_b = jnp.zeros((D,), dtype=jnp.float32)
        d_lr_u = 0.02 * jax.random.normal(ks[6], (D, R), dtype=jnp.float32)
        d_lr_v = 0.02 * jax.random.normal(ks[7], (R, D), dtype=jnp.float32)
        return {'u': u, 'a': a, 'b': b, 'c': c, 'd': d, 'gate_w': gate_w, 'gate_b': gate_b, 'd_lr_u': d_lr_u, 'd_lr_v': d_lr_v}
    _L0_attn_in = _L0_attn_setup()

    def _L0_ffn_setup():
        import jax, jax.numpy as jnp
        import numpy as np
        _FP4_LUT = jnp.array([0.0, 0.5, 1.0, 1.5, 2.0, 3.0, 4.0, 6.0, -0.0, -0.5, -1.0, -1.5, -2.0, -3.0, -4.0, -6.0], dtype=jnp.float32)
        GROUP_SIZE = 128
        EPS = 1e-06

        def _dequant_fp4(packed_i32, scales_f16, group_size):
            out_f, in_p = packed_i32.shape
            w = packed_i32.astype(jnp.uint32)
            shifts = jnp.arange(8, dtype=jnp.uint32) * 4
            nib = w[:, :, None] >> shifts & jnp.uint32(15)
            vals = _FP4_LUT[nib.astype(jnp.int32)].reshape(out_f, in_p * 8)
            s = scales_f16.astype(jnp.float32).T
            s_full = jnp.repeat(s, group_size, axis=1)
            return vals * s_full
        key = jax.random.key(seed)
        k1, k2, k3, k4, k5 = jax.random.split(key, 5)
        B, S, H, I = (4, 512, 512, 1408)
        x = jax.random.normal(k1, (B, S, H), dtype=jnp.float32)
        gate_up_packed = jax.random.randint(k2, (2 * I, H // 8), 0, 2147483647, dtype=jnp.int32)
        gate_up_scales = jax.random.uniform(k3, (H // GROUP_SIZE, 2 * I), dtype=jnp.float32).astype(jnp.float16)
        down_packed = jax.random.randint(k4, (H, I // 8), 0, 2147483647, dtype=jnp.int32)
        down_scales = jax.random.uniform(k5, (I // GROUP_SIZE, H), dtype=jnp.float32).astype(jnp.float16)
        return {'x': x, 'gate_up_packed': gate_up_packed, 'gate_up_scales': gate_up_scales, 'down_packed': down_packed, 'down_scales': down_scales}
    _L0_ffn_in = _L0_ffn_setup()
    _L0_c = _w((lambda *s: np.random.randn(*s).astype(np.float32) * 0.05)(4, 512))
    _L0_wmod = _w((lambda *s: np.random.randn(*s).astype(np.float32) * 0.05)(512, 6 * 512) * 512 ** (-0.5))
    _d = {'L0_attn_u': _L0_attn_in['u'], 'L0_attn_a': _L0_attn_in['a'], 'L0_attn_b': _L0_attn_in['b'], 'L0_attn_c': _L0_attn_in['c'], 'L0_attn_d': _L0_attn_in['d'], 'L0_attn_gate_w': _L0_attn_in['gate_w'], 'L0_attn_gate_b': _L0_attn_in['gate_b'], 'L0_attn_d_lr_u': _L0_attn_in['d_lr_u'], 'L0_attn_d_lr_v': _L0_attn_in['d_lr_v'], 'L0_ffn_gate_up_packed': _L0_ffn_in['gate_up_packed'], 'L0_ffn_gate_up_scales': _L0_ffn_in['gate_up_scales'], 'L0_ffn_down_packed': _L0_ffn_in['down_packed'], 'L0_ffn_down_scales': _L0_ffn_in['down_scales'], 'L0_c': _L0_c, 'L0_wmod': _L0_wmod}
    _x0 = _d['L0_attn_u']
    _d['L0_attn_u'] = jax.random.normal(jax.random.fold_in(jax.random.key(seed), 1), (4, 2048, 512), dtype=_x0.dtype)
    del _x0
    return _d

def reference(L0_attn_u, L0_attn_a, L0_attn_b, L0_attn_c, L0_attn_d, L0_attn_gate_w, L0_attn_gate_b, L0_attn_d_lr_u, L0_attn_d_lr_v, L0_ffn_gate_up_packed, L0_ffn_gate_up_scales, L0_ffn_down_packed, L0_ffn_down_scales, L0_c, L0_wmod):

    def _L0_attn_ref(u, a, b, c, d, gate_w, gate_b, d_lr_u, d_lr_v):
        import jax, jax.numpy as jnp
        import numpy as np
        B, T, D, R = (8, 512, 512, 4)
        Bs, Ts, Ds = u.shape
        rank = d_lr_u.shape[1]
        g = jax.nn.sigmoid(jnp.einsum('btd,ed->bte', u, gate_w) + gate_b)
        u_g = u * g
        aa = jnp.tanh(a)
        u_mean = jnp.mean(u_g, axis=1, keepdims=True)
        d_lr = u_mean @ d_lr_u @ d_lr_v / max(1.0, float(rank))
        d_eff = d + d_lr
        G = jnp.cumprod(jnp.broadcast_to(aa, (Ts, Ds)), axis=0)
        bu = b * u_g
        G_safe = G.at[0].set(jnp.maximum(G[0], 1e-06))
        z = bu / G_safe
        s = G * jnp.cumsum(z, axis=1)
        y = c * s + d_eff * u_g
        return y

    def _L0_ffn_ref(x, gate_up_packed, gate_up_scales, down_packed, down_scales):
        import jax, jax.numpy as jnp
        import numpy as np
        _FP4_LUT = jnp.array([0.0, 0.5, 1.0, 1.5, 2.0, 3.0, 4.0, 6.0, -0.0, -0.5, -1.0, -1.5, -2.0, -3.0, -4.0, -6.0], dtype=jnp.float32)
        GROUP_SIZE = 128
        EPS = 1e-06

        def _dequant_fp4(packed_i32, scales_f16, group_size):
            out_f, in_p = packed_i32.shape
            w = packed_i32.astype(jnp.uint32)
            shifts = jnp.arange(8, dtype=jnp.uint32) * 4
            nib = w[:, :, None] >> shifts & jnp.uint32(15)
            vals = _FP4_LUT[nib.astype(jnp.int32)].reshape(out_f, in_p * 8)
            s = scales_f16.astype(jnp.float32).T
            s_full = jnp.repeat(s, group_size, axis=1)
            return vals * s_full
        I = gate_up_packed.shape[0] // 2
        w_gu = _dequant_fp4(gate_up_packed, gate_up_scales, GROUP_SIZE)
        w_down = _dequant_fp4(down_packed, down_scales, GROUP_SIZE)
        gate_up = jnp.einsum('bsh,oh->bso', x, w_gu)
        gate, up = (gate_up[..., :I], gate_up[..., I:])
        h = jax.nn.silu(gate) * up
        y = jnp.einsum('bsi,hi->bsh', h, w_down)
        rms = jnp.sqrt(jnp.mean(y * y, axis=-1, keepdims=True) + EPS)
        return y / rms
    x = L0_attn_u
    mod = (_silu(L0_c) @ L0_wmod).reshape(L0_c.shape[0], 6, 1, -1)
    sa, ca, ga, sb, cb, gb = (mod[:, 0], mod[:, 1], mod[:, 2], mod[:, 3], mod[:, 4], mod[:, 5])
    ga = (2 * (ga >= 0) - 1) * jnp.maximum(jnp.abs(ga), 0.25)
    gb = (2 * (gb >= 0) - 1) * jnp.maximum(jnp.abs(gb), 0.25)
    h = _layernorm(x, axis=-1) * (1 + ca) + sa
    x = x + ga * _L0_attn_ref(h, L0_attn_a, L0_attn_b, L0_attn_c, L0_attn_d, L0_attn_gate_w, L0_attn_gate_b, L0_attn_d_lr_u, L0_attn_d_lr_v)
    h = _layernorm(x, axis=-1) * (1 + cb) + sb
    x = x + gb * _L0_ffn_ref(h, L0_ffn_gate_up_packed, L0_ffn_gate_up_scales, L0_ffn_down_packed, L0_ffn_down_scales)
    return x

_drawn_inputs = setup_inputs


def setup_inputs(seed=0):
    import zlib

    import numpy as np

    out = dict(_drawn_inputs(seed))
    spreads = {'L0_attn_gate_b': (0.0, 2.0)}
    factors = {'L0_attn_a': 8.0,
     'L0_attn_b': 8.0,
     'L0_attn_c': 8.0,
     'L0_attn_d': 8.0,
     'L0_attn_gate_w': 8.0,
     'L0_attn_d_lr_u': 64.0,
     'L0_attn_d_lr_v': 64.0}
    for name, (base, spread) in spreads.items():
        noise = np.random.default_rng([zlib.crc32(name.encode()), seed]).standard_normal(out[name].shape)
        drawn = base * np.exp(spread * noise) if base else spread * noise
        out[name] = jnp.asarray(drawn.astype(out[name].dtype))
    for name, factor in factors.items():
        out[name] = (out[name] * factor).astype(out[name].dtype)
    return out
```

```python
import numpy as np
import concourse.bass as bass
from concourse import mybir
from contextlib import ExitStack

F32 = mybir.dt.float32
F32R = mybir.dt.float32r
F16 = mybir.dt.float16
I32 = mybir.dt.int32
ALU = mybir.AluOpType
ACT = mybir.ActivationFunctionType

P = 128


def adaln_block_kernel(nc, u, a, b, c, d, gate_w, gate_b, d_lr_u, d_lr_v,
                       gu_packed, gu_scales, dn_packed, dn_scales, cond, wmod, out):
    NB, T, D = u.shape
    HID = gu_packed.shape[0] // 2
    RANK = d_lr_u.shape[1]
    NMOD = wmod.shape[1] // D
    TOK = 512
    NSUB = TOK // P
    TPB = T // TOK
    DC = D // P
    NCH = HID // P
    WPG = P // 8
    SHIFT_UP = 2.0 ** 14
    LN_EPS = 1e-5
    RMS_EPS = 1e-6
    SA, CA, GA, SB, CB, GB = range(6)

    xv = u.rearrange("b (j s p) d -> (b j) s p d", p=P, s=NSUB)
    ov = out.rearrange("b (j s p) d -> (b j) s p d", p=P, s=NSUB)

    ug_dram = nc.dram_tensor("ug_scratch", [NB * TPB, P, DC, TOK], F32).ap()
    xn_dram = nc.dram_tensor("xnew_scratch", [NB * TPB, NSUB, P, D], F32).ap()
    gb_dram = nc.dram_tensor("gb_scratch", [NB, D], F32).ap()

    with ExitStack() as ctx:
        def sb(name, shape, dt, scope=ctx):
            return scope.enter_context(nc.sbuf_tensor(name, shape, dt))

        def pb(name):
            return ctx.enter_context(nc.psum_tensor(name, [P, 512], F32))

        def sem(name):
            return ctx.enter_context(nc.semaphore(name))

        W1 = sb("gu_w1", [P, DC, 2 * HID], F32R)
        W2 = sb("gu_w2", [P, DC, 2 * HID], F32R)
        WG = sb("gate_wT", [P, DC, D], F32)
        chan = sb("chan", [P, DC, TOK], F32)
        xa = sb("xa", [P, 2, D], F32)
        xb = sb("xb", [P, 2, D], F32)
        two = sb("two", [P, 2, D], F32)
        ugo = sb("ugo", [P, 2, TOK], F32)
        ident = sb("ident", [P, P], F32)
        vec = sb("vec", [P, 5, DC], F32)
        modT = sb("modT", [P, NB, 5, DC], F32)
        modA = sb("modA", [P, 2, DC], F32)
        modP = sb("modP", [P, 2, DC], F32)
        coef = sb("coef", [P, 2, DC], F32)
        usum = sb("usum", [P, DC, TPB], F32)
        umean = sb("umean", [P, DC], F32)
        lru = sb("lru", [P, DC, RANK], F32)
        lrv = sb("lrv", [P, DC, RANK], F32)
        lrp = sb("lrp", [P, DC, RANK], F32)
        carry = sb("carry", [P, DC], F32)
        stat = sb("stat", [P, 4, 6], F32)
        mvA = sb("mvA", [P, 2, 2], F32)
        mvP = sb("mvP", [P, 2, 2], F32)
        rsA = sb("rsA", [P, 2, 2], F32)
        rsP = sb("rsP", [P, 2, 2], F32)
        ssq = sb("ssq", [P, NSUB], F32)
        rms = sb("rms", [P, NSUB, 2], F32)
        consts = sb("consts", [P, 3], F32)
        k_pow = consts[:, 0:1]
        k_eps = consts[:, 1:3]
        vecs = sb("vecs", [P, 5, DC], F32)
        aa = vecs[:, 0, :]
        f0 = vecs[:, 1, :]
        bc_ = vecs[:, 2, :]
        dlr = vecs[:, 3, :]
        deff = vecs[:, 4, :]
        cT = sb("cT", [P, DC, NB], F32)
        crow, csig = xb[0:NB, 0, :], xb[0:NB, 1, :]
        raw = xb
        gwr = chan

        with ExitStack() as early:
            wm = sb("wm", [P, 2, NMOD * D], F32, early)
            mrow = sb("mrow", [NB, NMOD * D], F32, early)
            mtmp = sb("mtmp", [NB, D], F32, early)
        V1 = sb("dn_w1", [P, NCH, D], F32R)
        V2 = sb("dn_w2", [P, NCH, D], F32R)
        with ExitStack() as early:
            gpk = sb("gu_words", [P, 2 * NCH, D // 8], I32, early)
            dpk = sb("dn_words", [P, DC, HID // 8], I32, early)
            SCW = DC * 2 * HID // 2
            scl = sb("scales", [P, 2, SCW], F16, early)
            nib = sb("nib", [P, 2 * HID], I32, early)
            ident16 = sb("ident16", [P, P], F16, early)
        X1 = sb("ffn_x1", [P, DC, TOK], F32R)
        X2 = sb("ffn_x2", [P, DC, TOK], F32R)
        hst = sb("ffn_x_next", [P, DC, TOK], F32)
        S = sb("silu_up", [P, 2, TOK], F32)
        H1 = sb("h1", [P, 2, TOK], F32R)
        H2 = sb("h2", [P, 2, TOK], F32R)
        yo = sb("y_out", [P, 2, D], F32)
        gbB = sb("gb_rows", [P, D], F32)

        bank = [pb("bank0"), pb("bank1")]
        gps = pb("gate_ps")
        ups = pb("up_ps")
        yps = [pb(f"y_ps{s}") for s in range(NSUB)]
        dq_banks = [gps, ups] + yps
        modps = [gps, ups] + yps

        S_ = {n: sem(n) for n in """
            cond_in vec_in lr_in gw_in gpk_in dpk_in ident_ok const_ok
            csig_ok silu_ok cT_mm cT_ok mod_mm mod_row modt_mm modt_ok mod_fix gb_saved
            gw_mm gw_ok gw_dve vec_tanh vec_fix
            dq_mm dq_top dq_nib dq_raw dq_w1 dq_w2
            a_stat a_mv a_eps a_rstd a_norm xT_mm hT_ok modA_ok gate_mm gate_sig ug_done
            um_done lr_mm lr_prod lr_sum d_eff d_tmp coef_ok
            p_first p_scan carry_ok p_mul yT_ok yT_mm x_new p_stat p_mv p_eps p_rstd p_norm hT2_mm modP_ok x_next
            x1_ok x2_ok g_mm u_mm sig_ok gs_ok h_ok h1_ok h2_ok d_mm
            y_mm sq_ok rms_a rms_ok y_used out_ok gb_in
        """.split()}
        wm_in = [sem(f"wm_in{i}") for i in range(2)]
        scl_in = [sem(f"scl_in{i}") for i in range(2)]
        xa_in = [sem(f"xa_in{i}") for i in range(2)]
        xb_in = [sem(f"xb_in{i}") for i in range(2)]
        ug_out = [sem(f"ug_out{i}") for i in range(2)]
        ug_in = sem("ug_in")
        xn_out = [sem(f"xn_out{i}") for i in range(2)]
        y_out = [sem(f"y_out{i}") for i in range(2)]

        START = 1
        STARTED = {"dve": [S_[k] for k in ("out_ok", "h2_ok", "gs_ok", "h_ok", "y_used")],
                   "pe": [S_[k] for k in ("y_mm", "d_mm")], "sp": y_out}

        GROUPS = [("gu", g, 1) for g in range(DC)] + [("dn", c_, min(4, NCH - c_)) for c_ in range(0, NCH, 4)]
        FIXES = 4
        UNITS = []
        for gi, (kind, c0, nc_) in enumerate(GROUPS):
            if kind == "gu":
                UNITS += [(gi, o, min(4, 2 * NCH - o), kind, c0, P * o) for o in range(0, 2 * NCH, 4)]
            else:
                UNITS += [(gi, c_, DC, kind, c0 + c_, 0) for c_ in range(nc_)]
        NU = len(UNITS)
        GROUP_END = [sum(1 for x in UNITS if x[0] <= gi) for gi in range(len(GROUPS))]
        SC_END = [GROUP_END[1], GROUP_END[3], NU]

        def dq_blocks(uu):
            gi, b0, nb_, kind, ch, col = UNITS[uu]
            n_ = GROUPS[gi][2]
            v = nib[:, :].bitcast(F16)
            for i in range(nb_):
                blk = b0 + i if kind == "gu" else i * n_ + b0
                yield v[:, 2 * P * blk + 1:2 * P * (blk + 1):2]

        def dq_dst(uu, which):
            gi, b0, nb_, kind, ch, col = UNITS[uu]
            w = (W1, W2) if kind == "gu" else (V1, V2)
            return w[which][:, ch, col:col + P * nb_]

        DQ_AT = [list(range(NU * k // 8, NU * (k + 1) // 8)) for k in range(8)]

        A_ORDER = [("xT", 0), ("xT", 1), ("xT", 2), ("xT", 3), ("gate", 0), ("gate", 1), ("gate", 2), ("gate", 3)]
        P_ORDER = [("yT", 0), ("yT", 1), ("yT", 2), ("hT2", 0), ("yT", 3), ("hT2", 1), ("hT2", 2), ("hT2", 3)]

        def freed(eng, piece, m, r, bt):
            kind, s = piece
            if kind == "xT":
                eng.wait_ge(S_["hT_ok"], 4 * m + s + 1)
            elif kind == "gate":
                eng.wait_ge(S_["gate_sig"], 4 * m + s + 1)
            elif kind == "lr":
                eng.wait_ge(S_["lr_prod"], bt + 1)
            elif kind == "yT":
                eng.wait_ge(S_["x_new"], 4 * r + s + 1)
            else:
                eng.wait_ge(S_["x_next"], 4 * r + s + 1)

        class Banks:
            def __init__(self):
                self.hist = []

            def take(self, eng, piece, m=None, r=None, bt=None):
                if len(self.hist) >= 2:
                    freed(eng, *self.hist[-2])
                if piece[0] == "lr":
                    self.hist[-2] = (piece, m, r, bt)
                    return bank[0]
                self.hist.append((piece, m, r, bt))
                return bank[(len(self.hist) - 1) % 2]

        def bank_of(piece, j, with_a):
            order = {"xT": A_ORDER, "gate": A_ORDER, "lr": [piece]}.get(piece[0], P_ORDER)
            return bank[order.index(piece) % 2]

        block = ctx.enter_context(nc.Block())

        @block.sync
        def _(sp):
            for first in STARTED["sp"]:
                sp.sem_inc(first, START)
            with nc.allow_non_contiguous_dma(reason="512-element vectors by channel"):
                sp.dma_start(crow, cond).then_inc(S_["cond_in"], 16)
                for k in range(2):
                    sp.dma_start(wm[:, k, :], wmod[P * k:P * (k + 1), :]).then_inc(wm_in[k], 16)
                for s in range(2):
                    sp.dma_start(xa[:, s, :], xv[0, s, :, :]).then_inc(xa_in[s], 16)
                for i, v in enumerate((a, b, c, d, gate_b)):
                    sp.dma_start(vec[:, i, :], v.rearrange("(c p) -> p c", p=P)).then_inc(S_["vec_in"], 16)
            sp.dma_start(gwr[:, :, :], gate_w.rearrange("(c p) d -> p c d", p=P)).then_inc(S_["gw_in"], 16)
            sp.dma_start(lru[:, :, :], d_lr_u.rearrange("(c p) r -> p c r", p=P)).then_inc(S_["lr_in"], 16)
            with nc.allow_non_contiguous_dma(reason="2048 elements by channel"):
                for c_ in range(DC):
                    sp.dma_start(lrv[:, c_, :], d_lr_v[:, P * c_:P * (c_ + 1)].rearrange("r p -> p r")
                                 ).then_inc(S_["lr_in"], 16)
            gsrc = gu_packed.rearrange("(c w j) k -> j w c k", w=WPG, j=8)
            for j in range(8):
                sp.dma_start(gpk[WPG * j:WPG * (j + 1), :, :], gsrc[j]).then_inc(S_["gpk_in"], 16)
            sp.dma_start(dpk[:, :, :], dn_packed.rearrange("(c p) k -> p c k", p=P)).then_inc(S_["dpk_in"], 16)
            gsc = gu_scales.rearrange("(h g) o -> h (g o)", h=2)
            for h in range(2):
                sp.dma_start(scl[:, h, :], gsc[h:h + 1, :].broadcast_to([P, SCW])).then_inc(scl_in[h], 16)
            for k in range(2, DC):
                sp.wait_ge(S_["mod_mm"], k - 1)
                sp.dma_start(wm[:, k % 2, :], wmod[P * k:P * (k + 1), :]).then_inc(wm_in[k % 2], 16)
            sp.wait_ge(S_["mod_fix"], 2 * FIXES)
            sp.dma_start(gb_dram, mrow[:, GB * D:(GB + 1) * D]).then_inc(S_["gb_saved"], 16)

            def load_x_attn(m, s):
                if not (isinstance(m, int) and 4 * m + s < 2):
                    sp.wait_ge(S_["xT_mm"], 4 * m + s - 1)
                sp.dma_start(xa[:, s % 2, :], xv[m, s, :, :]).then_inc(xa_in[s % 2], 16)

            def store_ug(m):
                for e in range(DC):
                    sp.wait_ge(S_["ug_done"], 4 * m + e + 1)
                    sp.dma_start(ug_dram[m, :, e, :], ugo[:, e % 2, :]).then_inc(ug_out[e % 2], 16)

            def load_ug(r, m):
                if m is not None:
                    sp.wait_ge(S_["ug_done"], 4 * m + 4)
                else:
                    sp.wait_ge(S_["yT_mm"], 4 * r)
                for k in range(2):
                    sp.wait_ge(ug_out[k], 32 * r + 32)
                sp.dma_start(chan[:, :, :], ug_dram[r, :, :, :]).then_inc(ug_in, 16)

            def load_x_prep(r, s, first):
                if s < 2:
                    if first:
                        sp.wait_ge(S_["dq_w2"], NU)
                    else:
                        sp.wait_ge(S_["out_ok"], START + 4 * r - 4)
                        sp.wait_ge(S_["p_norm"], 4 * r)
                        sp.wait_ge(xn_out[s % 2], 32 * r)
                else:
                    sp.wait_ge(xn_out[s % 2], 32 * r + 16)
                    sp.wait_ge(S_["p_norm"], 4 * r + s - 1)
                sp.dma_start(xb[:, s % 2, :], xv[r, s, :, :]).then_inc(xb_in[s % 2], 16)

            def store_x_new(r, s):
                sp.wait_ge(S_["x_new"], 4 * r + s + 1)
                sp.dma_start(xn_dram[r, s, :, :], xb[:, s % 2, :]).then_inc(xn_out[s % 2], 16)

            def load_x_final(n, s, r):
                if s < 2:
                    if r is not None:
                        sp.wait_ge(S_["p_norm"], 4 * r + s + 3)
                        sp.wait_ge(xn_out[s % 2], 32 * r + 32)
                    else:
                        sp.wait_ge(S_["out_ok"], START + 4 * n - 1 + s)
                        sp.wait_ge(xn_out[s % 2], 32 * n + 32)
                else:
                    sp.wait_ge(S_["out_ok"], START + 4 * n + s - 1)
                sp.dma_start(xb[:, s % 2, :], xn_dram[n, s, :, :]).then_inc(xb_in[s % 2], 16)

            def store_out(n, s):
                sp.wait_ge(S_["out_ok"], START + 4 * n + s + 1)
                sp.dma_start(ov[n, s, :, :], yo[:, s % 2, :]).then_inc(y_out[s % 2], 16)

            def prep(r, m, first=False):
                load_ug(r, m)
                load_x_prep(r, 0, first)
                load_x_prep(r, 1, first)
                for s in range(NSUB):
                    store_x_new(r, s)
                    if s < 2:
                        load_x_prep(r, s + 2, first)

            for m in range(TPB):
                for s in range(NSUB):
                    if m or s > 1:
                        load_x_attn(m, s)
                    if m == 1 and s == 3:
                        sp.wait_ge(S_["dq_raw"], SC_END[0])
                        dsc = dn_scales.rearrange("g o -> (g o)").unsqueeze(0)
                        sp.dma_start(scl[:, 0, :], dsc.broadcast_to([P, SCW])).then_inc(scl_in[0], 16)
                store_ug(m)
            prep(0, TPB - 1, first=True)

            def step(n, j, with_a, with_p):
                m, r = n + TPB, n + 1
                if j == 0:
                    if not isinstance(n, int) or n > 0:
                        sp.wait_ge(S_["out_ok"], START + 4 * n)
                    sp.wait_ge(S_["dq_w2"], NU)
                    sp.wait_ge(S_["gb_saved"], 16)
                    bt = n // TPB if isinstance(n, int) else (n_batch[0])
                    sp.dma_start(gbB[:, :], gb_dram[bt:bt + 1, :].broadcast_to([P, D]) if isinstance(bt, int)
                                 else gb_dram[bass.ds(bt, 1), :].broadcast_to([P, D])).then_inc(S_["gb_in"], 16)
                if with_a:
                    for s in range(NSUB):
                        load_x_attn(m, s)
                    store_ug(m)
                if with_p:
                    prep(r, m if with_a else None, first=(isinstance(n, int) and n == 0))
                load_x_final(n, 0, r if with_p else None)
                load_x_final(n, 1, r if with_p else None)
                for s in range(NSUB):
                    store_out(n, s)
                    if s < 2:
                        load_x_final(n, s + 2, None)

            n_batch = [None]
            with sp.Fori(0, NB - 1) as bt:
                n_batch[0] = bt
                for j in range(TPB):
                    step(TPB * bt + j, j, True, True)
            for j in range(TPB):
                step(TPB * (NB - 1) + j, j, False, j < TPB - 1)
            for k in range(2):
                sp.wait_ge(y_out[k], START + 32 * NB * TPB)
                sp.wait_ge(xn_out[k], 32 * NB * TPB)
                sp.wait_ge(ug_out[k], 32 * NB * TPB)

        @block.gpsimd
        def _(pool):
            nc.gpsimd.memset(ident[:, :], 0.0).then_inc(S_["const_ok"], 1)
            nc.gpsimd.memset(k_pow[:, :], -0.5).then_inc(S_["const_ok"], 1)
            nc.gpsimd.memset(k_eps[:, 0:1], LN_EPS).then_inc(S_["const_ok"], 1)
            nc.gpsimd.memset(k_eps[:, 1:2], RMS_EPS * SHIFT_UP ** -2).then_inc(S_["const_ok"], 1)
            pool.wait_ge(S_["const_ok"], 4)
            nc.gpsimd.affine_select(out=ident[:, :], in_=ident[:, :], compare_op=ALU.not_equal, fill=1.0,
                                    base=0, pattern=[[-1, P]], channel_multiplier=1).then_inc(S_["ident_ok"], 1)
            pool.wait_ge(S_["ident_ok"], 1)
            nc.gpsimd.tensor_copy(ident16[:, :], ident[:, :]).then_inc(S_["ident_ok"], 1)

            def rstd(mv, rs, s, got, mid, done, idx):
                pool.wait_ge(S_[got], idx + 1)
                nc.gpsimd.tensor_tensor(rs[:, s % 2, 0:1], mv[:, s % 2, 1:2], k_eps[:, 0:1],
                                        ALU.add).then_inc(S_[mid], 1)
                pool.wait_ge(S_[mid], idx + 1)
                nc.gpsimd.tensor_tensor(rs[:, s % 2, 1:2], rs[:, s % 2, 0:1], k_pow[:, :],
                                        ALU.pow).then_inc(S_[done], 1)

            def rstd_a(m, s):
                rstd(mvA, rsA, s, "a_mv", "a_eps", "a_rstd", 4 * m + s)

            def rstd_p(r, s):
                rstd(mvP, rsP, s, "p_mv", "p_eps", "p_rstd", 4 * r + s)

            def final(n):
                for s in range(NSUB):
                    pool.wait_ge(S_["sq_ok"], 4 * n + s + 1)
                    nc.gpsimd.tensor_tensor(rms[:, s, 0:1], ssq[:, s:s + 1], k_eps[:, 1:2],
                                            ALU.add).then_inc(S_["rms_a"], 1)
                    pool.wait_ge(S_["rms_a"], 4 * n + s + 1)
                    nc.gpsimd.tensor_tensor(rms[:, s, 1:2], rms[:, s, 0:1], k_pow[:, :],
                                            ALU.pow).then_inc(S_["rms_ok"], 1)

            for m in range(TPB):
                for s in range(NSUB):
                    rstd_a(m, s)
            for s in range(NSUB):
                rstd_p(0, s)

            def step(n, with_a, with_p):
                if with_a:
                    for s in range(NSUB):
                        rstd_a(n + TPB, s)
                if with_p:
                    for s in range(NSUB):
                        rstd_p(n + 1, s)
                final(n)

            with pool.Fori(0, NB - 1) as bt:
                for j in range(TPB):
                    step(TPB * bt + j, True, True)
            for j in range(TPB):
                step(TPB * (NB - 1) + j, False, j < TPB - 1)

        @block.scalar
        def _(act):
            def batch_cols(dst, rows, bt, done):
                for i, row in enumerate(rows):
                    src = modT[:, bass.ds(bt, 1), row, :] if not isinstance(bt, int) else modT[:, bt:bt + 1, row, :]
                    ins = nc.scalar.activation(dst[:, i:i + 1, :], src, ACT.Copy)
                ins.then_inc(S_[done], 1)
                act.wait_ge(S_[done], bt + 1)

            def x_evac(m, s, j, first_piece_wait):
                if j == 0 and s == 0:
                    batch_cols(modA, (SA, CA), bt_of(m), "modA_ok")
                act.wait_ge(S_["xT_mm"], 4 * m + s + 1)
                if s == 0 and first_piece_wait is not None:
                    act.wait_ge(S_["yT_mm"], first_piece_wait)
                if s == 0 and isinstance(m, int) and m in range(1, TPB):
                    act.wait_ge(S_["ug_done"], 4 * m)
                src = bank_of(("xT", s), j, True)
                for c_ in range(DC):
                    ins = nc.scalar.activation(chan[:, c_, P * s:P * (s + 1)], src[:, P * c_:P * (c_ + 1)],
                                               ACT.Identity, bias=modA[:, 0, c_:c_ + 1], scale=modA[:, 1, c_:c_ + 1])
                ins.then_inc(S_["hT_ok"], 1)

            def gate_sig(m, e):
                act.wait_ge(S_["gate_mm"], 4 * m + e + 1)
                if e < 2:
                    if isinstance(m, int):
                        if m:
                            act.wait_ge(S_["ug_done"], 4 * m + e - 1)
                    else:
                        act.wait_ge(S_["hT2_mm"], 4 * (m - TPB) + 4)
                else:
                    act.wait_ge(S_["ug_done"], 4 * m + e - 1)
                nc.scalar.activation(two[:, e % 2, :], bank_of(("gate", e), 0, True)[:, :], ACT.Sigmoid,
                                     bias=vec[:, 4, e:e + 1]).then_inc(S_["gate_sig"], 1)

            def h_evac(r, s, j_r, ffn_before):
                if j_r == 0 and s == 0:
                    batch_cols(modP, (SB, CB), bt_of(r), "modP_ok")
                act.wait_ge(S_["hT2_mm"], 4 * r + s + 1)
                if s == 0 and ffn_before:
                    act.wait_ge(S_["x2_ok"], 4 * r)
                src = bank_of(("hT2", s), 0, True)
                for c_ in range(DC):
                    ins = nc.scalar.activation(hst[:, c_, P * s:P * (s + 1)], src[:, P * c_:P * (c_ + 1)],
                                               ACT.Identity, bias=modP[:, 0, c_:c_ + 1], scale=modP[:, 1, c_:c_ + 1])
                ins.then_inc(S_["x_next"], 1)

            def split_x(r, c_, ffn_before):
                if c_ == 0:
                    act.wait_ge(S_["x_next"], 4 * r + 4)
                    if ffn_before:
                        act.wait_ge(S_["u_mm"], NCH * r)
                nc.scalar.activation(X1[:, c_, :], hst[:, c_, :], ACT.Copy).then_inc(S_["x1_ok"], 1)

            def chunk_sig(n, i):
                q = NCH * n + i
                act.wait_ge(S_["g_mm"], q + 1)
                act.wait_ge(S_["h2_ok"], START + (q - 1 if i else q))
                nc.scalar.activation(S[:, i % 2, :], gps[:, :], ACT.Sigmoid, scale=SHIFT_UP).then_inc(S_["sig_ok"], 1)

            def chunk_h1(n, i):
                q = NCH * n + i
                act.wait_ge(S_["h_ok"], START + q + 1)
                if i == 0:
                    act.wait_ge(S_["y_mm"], START + 4 * n)
                else:
                    act.wait_ge(S_["d_mm"], START + (NCH - 1) * n + i - 1)
                nc.scalar.activation(H1[:, i % 2, :], S[:, i % 2, :], ACT.Copy).then_inc(S_["h1_ok"], 1)

            def final(n):
                for s in range(NSUB):
                    act.wait_ge(S_["y_mm"], START + 4 * n + s + 1)
                    if s < 2:
                        if not (isinstance(n, int) and n == 0):
                            act.wait_ge(y_out[s % 2], START + 32 * n)
                    else:
                        act.wait_ge(y_out[s % 2], START + 32 * n + 16)
                    nc.scalar.activation(yo[:, s % 2, :], yps[s][:, :], ACT.Square, scale=float(D) ** -0.5,
                                         accum_out=ssq[:, s:s + 1]).then_inc(S_["sq_ok"], 1)

            cur = {}

            def bt_of(t):
                return t // TPB if isinstance(t, int) else cur["bt"] + 1

            act.wait_ge(S_["cond_in"], 16)
            nc.scalar.activation(csig, crow, ACT.Sigmoid).then_inc(S_["csig_ok"], 1)
            act.wait_ge(S_["vec_in"], 80)
            nc.scalar.activation(aa[:, :], vec[:, 0, :], ACT.Tanh).then_inc(S_["vec_tanh"], 1)
            act.wait_ge(S_["cT_mm"], 1)
            nc.scalar.activation(cT[:, :, :], bank[0][:, 0:DC * NB].rearrange("p (c b) -> p c b", b=NB),
                                 ACT.Copy).then_inc(S_["cT_ok"], 1)
            act.wait_ge(S_["mod_mm"], DC)
            for i in range(NMOD):
                dst, src = mrow[:, D * i:D * (i + 1)], modps[i][0:NB, :]
                if i in (SB, CB):
                    dst = dst.rearrange("b (c j w) -> b c w j", j=8, w=WPG)
                    src = src.rearrange("b (c w j) -> b c w j", j=8, w=WPG)
                nc.scalar.activation(dst, src, ACT.Identity,
                                     bias=1.0 if i in (CA, CB) else 0.0).then_inc(S_["mod_row"], 1)
            act.wait_ge(S_["modt_mm"], 1)
            nc.scalar.activation(modT[:, :, :, :],
                                 bank[0][:, 0:5 * DC * NB].rearrange("p (k c b) -> p b k c", b=NB, c=DC),
                                 ACT.Copy).then_inc(S_["modt_ok"], 1)
            act.wait_ge(S_["modt_ok"], 1)
            for k in range(DC):
                act.wait_ge(S_["gw_mm"], k + 1)
                nc.scalar.activation(WG[:, k, :], bank[k % 2][:, :], ACT.Copy).then_inc(S_["gw_ok"], 1)

            def dq(uu):
                if uu == GROUP_END[DC - 1]:
                    act.wait_ge(S_["gb_saved"], 16)
                act.wait_ge(S_["dq_raw"], uu + 1)
                nc.scalar.activation(dq_dst(uu, 0), raw[:, uu % 2, 0:P * UNITS[uu][2]],
                                     ACT.Copy).then_inc(S_["dq_w1"], 1)

            for m in range(TPB):
                for s in range(NSUB):
                    x_evac(m, s, m, None)
                for uu in DQ_AT[2 * m]:
                    dq(uu)
                for e in range(DC):
                    gate_sig(m, e)
                for uu in DQ_AT[2 * m + 1]:
                    dq(uu)
            act.wait_ge(S_["dq_w2"], NU)
            for s in range(NSUB):
                h_evac(0, s, 0, False)
            for c_ in range(DC):
                split_x(0, c_, False)

            def step(n, j, with_a, with_p):
                m, r = n + TPB, n + 1
                for i in range(NCH):
                    chunk_sig(n, i)
                    chunk_h1(n, i)
                    if with_a:
                        if i in (1, 2):
                            for s in (2 * i - 2, 2 * i - 1):
                                x_evac(m, s, j, 4 * n + 4)
                        if i in (3, 4):
                            for e in (2 * i - 6, 2 * i - 5):
                                gate_sig(m, e)
                    if with_p:
                        for s in {8: (0,), 9: (1,), 10: (2, 3)}.get(i, ()):
                            h_evac(r, s, (j + 1) % TPB, True)
                if with_p:
                    for c_ in range(DC):
                        split_x(r, c_, True)
                final(n)

            with act.Fori(0, NB - 1) as bt:
                cur["bt"] = bt
                for j in range(TPB):
                    step(TPB * bt + j, j, True, True)
            for j in range(TPB):
                step(TPB * (NB - 1) + j, j, False, j < TPB - 1)

        @block.vector
        def _(dve):
            for first in STARTED["dve"]:
                dve.sem_inc(first, START)

            def norm_rows(m, h):
                s0 = 2 * h
                k = 4 * m + s0
                dve.wait_ge(S_["a_norm"], k)
                dve.wait_ge(S_["a_mv"], k)
                dve.wait_ge(xa_in[0], 32 * m + 16 * h + 16)
                nc.vector.bn_stats(stat[:, 0, :], xa[:, 0, :]).then_inc(S_["a_stat"], 1)
                dve.wait_ge(xa_in[1], 32 * m + 16 * h + 16)
                dve.wait_ge(S_["a_stat"], k + 1)
                nc.vector.bn_stats(stat[:, 1, :], xa[:, 1, :]).then_inc(S_["a_stat"], 1)
                nc.vector.bn_aggr(mvA[:, 0, :], stat[:, 0, :]).then_inc(S_["a_mv"], 1)
                dve.wait_ge(S_["a_stat"], k + 2)
                norm_a(m, s0)
                nc.vector.bn_aggr(mvA[:, 1, :], stat[:, 1, :]).then_inc(S_["a_mv"], 1)
                norm_a(m, s0 + 1)

            def norm_a(m, s):
                k = 4 * m + s
                dve.wait_ge(S_["a_rstd"], k + 1)
                nc.vector.tensor_scalar(xa[:, s % 2, :], xa[:, s % 2, :], mvA[:, s % 2, 0:1], rsA[:, s % 2, 1:2],
                                        ALU.subtract, ALU.mult).then_inc(S_["a_norm"], 1)

            def gated(m, e, j):
                k = 4 * m + e
                dve.wait_ge(S_["gate_sig"], k + 1)
                if e < 2:
                    if not (isinstance(m, int) and m == 0):
                        dve.wait_ge(ug_out[e % 2], 32 * m)
                else:
                    dve.wait_ge(ug_out[e % 2], 32 * m + 16)
                nc.vector.scalar_tensor_tensor(out=ugo[:, e % 2, :], in0=chan[:, e, :], scalar=1.0,
                                               in1=two[:, e % 2, :], op0=ALU.mult, op1=ALU.mult,
                                               accum_out=usum[:, e, j:j + 1]).then_inc(S_["ug_done"], 1)

            def u_total(bt, m):
                dve.wait_ge(S_["ug_done"], 4 * m + 4)
                nc.vector.reduce_sum(umean[:, :], usum[:, :, :], mybir.AxisListType.X).then_inc(S_["um_done"], 1)

            def new_coef(bt):
                dve.wait_ge(S_["lr_in"], 16 * (1 + DC))
                dve.wait_ge(S_["lr_mm"], bt + 1)
                by_rank = bank_of(("lr", 0), 0, True)[:, 0:RANK].unsqueeze(1).broadcast_to([P, DC, RANK])
                nc.vector.tensor_tensor(lrp[:, :, :], by_rank, lrv[:, :, :], ALU.mult).then_inc(S_["lr_prod"], 1)
                dve.wait_ge(S_["lr_prod"], bt + 1)
                nc.vector.reduce_sum(dlr[:, :], lrp[:, :, :], mybir.AxisListType.X).then_inc(S_["lr_sum"], 1)
                dve.wait_ge(S_["lr_sum"], bt + 1)
                nc.vector.scalar_tensor_tensor(out=deff[:, :], in0=dlr[:, :],
                                               scalar=1.0 / (T * max(1.0, float(RANK))), in1=vec[:, 3, :],
                                               op0=ALU.mult, op1=ALU.add).then_inc(S_["d_eff"], 1)
                ga = modT[:, bt, GA, :] if isinstance(bt, int) else \
                    modT[:, bass.ds(bt, 1), GA, :].rearrange("p o c -> p (o c)")
                nc.vector.tensor_tensor(coef[:, 0, :], bc_[:, :], ga, ALU.mult).then_inc(S_["d_tmp"], 1)
                dve.wait_ge(S_["d_eff"], bt + 1)
                nc.vector.tensor_tensor(coef[:, 1, :], deff[:, :], ga, ALU.mult).then_inc(S_["coef_ok"], 1)

            def scan(r, e, j):
                k = 4 * r + e
                if e == 0:
                    dve.wait_ge(ug_in, 16 * r + 16)
                    bt = bt_of(r)
                    dve.wait_ge(S_["coef_ok"], bt + 1)
                    dve.wait_ge(S_["d_tmp"], bt + 1)
                if e < 2:
                    if not (isinstance(r, int) and r == 0):
                        dve.wait_ge(S_["hT2_mm"], 4 * r)
                    dve.wait_ge(S_["ug_done"], scan_floor(r, e))
                else:
                    dve.wait_ge(S_["yT_ok"], k - 1)
                st = two[:, e % 2, :]
                if j == 0:
                    bt = bt_of(r)
                    nc.vector.tensor_tensor(st[:, 0:1], chan[:, e, 0:1], f0[:, e:e + 1],
                                            ALU.mult).then_inc(S_["p_first"], 1)
                    dve.wait_ge(S_["p_first"], 4 * bt + e + 1)
                    nc.vector.tensor_tensor_scan(st[:, 1:TOK], aa[:, e:e + 1].broadcast_to([P, TOK - 1]),
                                                 chan[:, e, 1:TOK], st[:, 0:1], ALU.mult, ALU.add
                                                 ).then_inc(S_["p_scan"], 1)
                else:
                    dve.wait_ge(S_["carry_ok"], 4 * (r - 1) + e + 1)
                    nc.vector.tensor_tensor_scan(st, aa[:, e:e + 1].broadcast_to([P, TOK]), chan[:, e, :],
                                                 carry[:, e:e + 1], ALU.mult, ALU.add).then_inc(S_["p_scan"], 1)
                dve.wait_ge(S_["p_scan"], k + 1)
                nc.vector.tensor_copy(carry[:, e:e + 1], st[:, TOK - 1:TOK]).then_inc(S_["carry_ok"], 1)
                nc.vector.tensor_scalar(chan[:, e, :], chan[:, e, :], coef[:, 1, e:e + 1], None,
                                        ALU.mult).then_inc(S_["p_mul"], 1)
                dve.wait_ge(S_["p_mul"], k + 1)
                nc.vector.scalar_tensor_tensor(out=chan[:, e, :], in0=st, scalar=coef[:, 0, e:e + 1],
                                               in1=chan[:, e, :], op0=ALU.mult, op1=ALU.add
                                               ).then_inc(S_["yT_ok"], 1)

            def scan_floor(r, e):
                if isinstance(r, int):
                    return 4 * min(r + TPB, NB * TPB) if r else 4 * TPB
                return 4 * (r + TPB)

            def add_x(r, s, after=None):
                k = 4 * r + s
                dve.wait_ge(S_["yT_mm"], k + 1)
                finals = r - 1
                cnt = 32 * r + 16 * (s // 2) + 16
                if not (isinstance(r, int) and r == 0):
                    cnt = cnt + 32 * finals
                dve.wait_ge(xb_in[s % 2], cnt)
                if after is not None:
                    dve.wait_ge(S_["p_stat"], 4 * r + after + 1)
                nc.vector.tensor_tensor(xb[:, s % 2, :], bank_of(("yT", s), 0, True)[:, :], xb[:, s % 2, :],
                                        ALU.add).then_inc(S_["x_new"], 1)
                if after is not None:
                    aggr_p(r, after)
                dve.wait_ge(S_["x_new"], k + 1)
                if not (isinstance(r, int) and k < 2):
                    dve.wait_ge(S_["p_mv"], k - 1)
                    dve.wait_ge(S_["p_norm"], k - 1)
                nc.vector.bn_stats(stat[:, 2 + s % 2, :], xb[:, s % 2, :]).then_inc(S_["p_stat"], 1)

            def aggr_p(r, s):
                nc.vector.bn_aggr(mvP[:, s % 2, :], stat[:, 2 + s % 2, :]).then_inc(S_["p_mv"], 1)

            def norm_p(r, s, after=None):
                k = 4 * r + s
                dve.wait_ge(S_["p_rstd"], k + 1)
                if s < 2:
                    dve.wait_ge(S_["yT_ok"], 4 * r + 4)
                else:
                    dve.wait_ge(S_["hT2_mm"], k - 1)
                if after is not None:
                    dve.wait_ge(S_["p_stat"], 4 * r + after + 1)
                dst = two[:, s % 2, :].rearrange("p (g j w) -> p g w j", j=8, w=WPG)
                src = xb[:, s % 2, :].rearrange("p (g w j) -> p g w j", j=8, w=WPG)
                nc.vector.tensor_scalar(dst, src, mvP[:, s % 2, 0:1], rsP[:, s % 2, 1:2],
                                        ALU.subtract, ALU.mult).then_inc(S_["p_norm"], 1)
                if after is not None:
                    aggr_p(r, after)

            def split_x(r, c_):
                dve.wait_ge(S_["x1_ok"], 4 * r + c_ + 1)
                nc.vector.tensor_tensor(X2[:, c_, :], hst[:, c_, :], X1[:, c_, :].bitcast(F32),
                                        ALU.subtract).then_inc(S_["x2_ok"], 1)

            def chunk_h(n, i):
                q = NCH * n + i
                s_ = S[:, i % 2, :]
                dve.wait_ge(S_["sig_ok"], q + 1)
                nc.vector.scalar_tensor_tensor(out=s_, in0=gps[:, :], scalar=SHIFT_UP, in1=s_,
                                               op0=ALU.mult, op1=ALU.mult).then_inc(S_["gs_ok"], 1)
                dve.wait_ge(S_["u_mm"], q + 1)
                dve.wait_ge(S_["gs_ok"], START + q + 1)
                nc.vector.scalar_tensor_tensor(out=s_, in0=ups[:, :], scalar=SHIFT_UP, in1=s_,
                                               op0=ALU.mult, op1=ALU.mult).then_inc(S_["h_ok"], 1)

            def chunk_h2(n, i):
                q = NCH * n + i
                dve.wait_ge(S_["h1_ok"], q + 1)
                nc.vector.tensor_tensor(H2[:, i % 2, :], S[:, i % 2, :], H1[:, i % 2, :].bitcast(F32),
                                        ALU.subtract).then_inc(S_["h2_ok"], 1)

            def final(n, bt):
                for s in range(NSUB):
                    k = 4 * n + s
                    dve.wait_ge(S_["rms_ok"], k + 1)
                    if s == 0:
                        dve.wait_ge(S_["gb_in"], 16 * bt + 16)
                    nc.vector.scalar_tensor_tensor(out=yo[:, s % 2, :], in0=yps[s][:, :], scalar=rms[:, s, 1:2],
                                                   in1=gbB[:, :], op0=ALU.mult, op1=ALU.mult
                                                   ).then_inc(S_["y_used"], 1)
                    preps = n + 2
                    if isinstance(n, int):
                        preps = min(n + 2, NB * TPB)
                    dve.wait_ge(xb_in[s % 2], 32 * preps + 32 * n + 16 * (s // 2) + 16)
                    dve.wait_ge(S_["y_used"], START + k + 1)
                    nc.vector.tensor_tensor(yo[:, s % 2, :], yo[:, s % 2, :], xb[:, s % 2, :],
                                            ALU.add).then_inc(S_["out_ok"], 1)

            cur = {}

            def bt_of(t):
                return t // TPB if isinstance(t, int) else cur["bt_" + str(cur["which"])]

            dve.wait_ge(S_["csig_ok"], 1)
            nc.vector.tensor_tensor(csig, csig, crow, ALU.mult).then_inc(S_["silu_ok"], 1)
            norm_rows(0, 0)
            dve.wait_ge(S_["vec_tanh"], 1)
            nc.vector.tensor_scalar(f0[:, :], aa[:, :], 1e-6, None, ALU.max).then_inc(S_["vec_fix"], 1)
            nc.vector.tensor_tensor(bc_[:, :], vec[:, 1, :], vec[:, 2, :], ALU.mult).then_inc(S_["vec_fix"], 1)
            dve.wait_ge(S_["vec_fix"], 2)
            nc.vector.reciprocal(f0[:, :], f0[:, :]).then_inc(S_["vec_fix"], 1)
            dve.wait_ge(S_["vec_fix"], 3)
            nc.vector.tensor_tensor(f0[:, :], f0[:, :], aa[:, :], ALU.mult).then_inc(S_["vec_fix"], 1)
            dve.wait_ge(S_["vec_fix"], 4)
            for k, row in enumerate((GA, GB)):
                g_ = mrow[:, D * row:D * (row + 1)]
                dve.wait_ge(S_["mod_row"], NMOD)
                nc.vector.tensor_scalar(mtmp[:, :], g_, 0.0, 2.0, ALU.is_ge, ALU.mult).then_inc(S_["mod_fix"], 1)
                dve.wait_ge(S_["mod_fix"], FIXES * k + 1)
                nc.vector.tensor_scalar(mtmp[:, :], mtmp[:, :], 1.0, None, ALU.subtract).then_inc(S_["mod_fix"], 1)
                nc.vector.scalar_tensor_tensor(out=g_, in0=g_, scalar=-1.0, in1=g_,
                                               op0=ALU.mult, op1=ALU.max).then_inc(S_["mod_fix"], 1)
                dve.wait_ge(S_["mod_fix"], FIXES * k + 3)
                nc.vector.scalar_tensor_tensor(out=g_, in0=g_, scalar=0.25, in1=mtmp[:, :],
                                               op0=ALU.max, op1=ALU.mult).then_inc(S_["mod_fix"], 1)
                dve.wait_ge(S_["mod_fix"], FIXES * (k + 1))

            def dq_unpack(gi):
                kind, c0, n_ = GROUPS[gi]
                if gi == 0:
                    dve.wait_ge(S_["gpk_in"], 16 * 8)
                    dve.wait_ge(S_["dpk_in"], 16)
                else:
                    dve.wait_ge(S_["dq_mm"], GROUP_END[gi - 1])
                if kind == "gu":
                    words = gpk[:, :, WPG * c0:WPG * (c0 + 1)]
                    out_ = nib[:, :].rearrange("p (o j w) -> p o j w", j=8, w=WPG)
                    size = 2 * HID
                else:
                    words = dpk[:, :, WPG * c0:WPG * (c0 + n_)].rearrange("p h (c w) -> p h c w", w=WPG)
                    size = DC * n_ * P
                    out_ = nib[:, 0:size].rearrange("p (h c j w) -> p h c j w", c=n_, j=8, w=WPG)
                for j in range(8):
                    ins = nc.vector.tensor_scalar(out_[:, :, j, :] if kind == "gu" else out_[:, :, :, j, :], words,
                                                  28 - 4 * j, 3, ALU.logical_shift_left, ALU.arith_shift_right)
                ins.then_inc(S_["dq_top"], 1)
                dve.wait_ge(S_["dq_top"], gi + 1)
                nc.vector.tensor_scalar(nib[:, 0:size], nib[:, 0:size], -0x72000000, None,
                                        ALU.bitwise_and).then_inc(S_["dq_nib"], 1)

            def dq(uu):
                gi, b0, nb_, kind, ch, col = UNITS[uu]
                if uu == 0 or UNITS[uu - 1][0] != gi:
                    dq_unpack(gi)
                if uu >= 2:
                    dve.wait_ge(S_["dq_w2"], uu - 1)
                part = [uu < e_ for e_ in SC_END].index(True)
                at = (2 * HID * (ch % 2) + col) if kind == "gu" else D * ch
                dve.wait_ge(scl_in[part % 2], 16 * (part // 2) + 16)
                dve.wait_ge(S_["dq_mm"], uu + 1)
                scale, dst = scl[:, part % 2, at:at + P * nb_], raw[:, uu % 2, 0:P * nb_]
                val = dq_banks[uu % 6][:, :].bitcast(F16)[:, 0:P * nb_]
                if kind == "gu":
                    scale = scale.rearrange("p (c w j) -> p c j w", w=WPG, j=8)
                    val = val.rearrange("p (c j w) -> p c j w", w=WPG, j=8)
                    dst = dst.rearrange("p (c j w) -> p c j w", w=WPG, j=8)
                nc.vector.tensor_tensor(dst, val, scale, ALU.mult).then_inc(S_["dq_raw"], 1)
                if uu >= 1:
                    dq_low(uu - 1)

            def dq_low(uu):
                dve.wait_ge(S_["dq_w1"], uu + 1)
                nc.vector.tensor_tensor(dq_dst(uu, 1), raw[:, uu % 2, 0:P * UNITS[uu][2]], dq_dst(uu, 0).bitcast(F32),
                                        ALU.subtract).then_inc(S_["dq_w2"], 1)

            for m in range(TPB):
                if m:
                    norm_rows(m, 0)
                norm_rows(m, 1)
                for uu in DQ_AT[2 * m]:
                    dq(uu)
                for e in range(DC):
                    gated(m, e, m)
                for uu in DQ_AT[2 * m + 1]:
                    dq(uu)
            dq_low(NU - 1)
            cur["which"] = "p"
            u_total(0, TPB - 1)
            new_coef(0)
            for e in range(DC):
                scan(0, e, 0)
            add_x(0, 0)
            add_x(0, 1, after=0)
            norm_p(0, 0, after=1)
            add_x(0, 2)
            norm_p(0, 1, after=2)
            add_x(0, 3)
            norm_p(0, 2, after=3)
            norm_p(0, 3)
            for c_ in range(DC):
                split_x(0, c_)

            def step(n, j, bt, with_a, with_p):
                m, r = n + TPB, n + 1
                cur["bt_p"] = bt + 1 if j == TPB - 1 else bt
                for i in range(NCH):
                    chunk_h(n, i)
                    chunk_h2(n, i)
                    if with_a:
                        if i in (0, 1):
                            norm_rows(m, i)
                        if i in (3, 4):
                            for e in (2 * i - 6, 2 * i - 5):
                                gated(m, e, j)
                        if i == 4 and j == TPB - 1:
                            u_total(bt + 1, m)
                        if i == 6 and j == TPB - 1:
                            new_coef(bt + 1)
                    if with_p:
                        if i in ((6, 7) if j == TPB - 1 else (5, 6)):
                            k = i - 6 if j == TPB - 1 else i - 5
                            scan(r, 2 * k, (j + 1) % TPB)
                            scan(r, 2 * k + 1, (j + 1) % TPB)
                        if i == 7:
                            add_x(r, 0)
                            add_x(r, 1, after=0)
                            norm_p(r, 0, after=1)
                        if i == 8:
                            add_x(r, 2)
                            norm_p(r, 1, after=2)
                        if i == 9:
                            add_x(r, 3)
                            norm_p(r, 2, after=3)
                            norm_p(r, 3)
                if with_p:
                    for c_ in range(DC):
                        split_x(r, c_)
                final(n, bt)

            with dve.Fori(0, NB - 1) as bt:
                for j in range(TPB):
                    step(TPB * bt + j, j, bt, True, True)
            for j in range(TPB):
                step(TPB * (NB - 1) + j, j, NB - 1, False, j < TPB - 1)

        @block.tensor
        def _(pe):
            for first in STARTED["pe"]:
                pe.sem_inc(first, START)

            def attn_T(bk, m, s):
                dst = bk.take(pe, ("xT", s), m=m)
                pe.wait_ge(S_["a_norm"], 4 * m + s + 1)
                for c_ in range(DC):
                    ins = nc.tensor.transpose(dst[:, P * c_:P * (c_ + 1)], xa[:, s % 2, P * c_:P * (c_ + 1)], ident[:, :])
                ins.then_inc(S_["xT_mm"], 1)

            def gate(bk, m, e):
                dst = bk.take(pe, ("gate", e), m=m)
                pe.wait_ge(S_["hT_ok"], 4 * m + 4)
                for k in range(DC):
                    ins = nc.tensor.matmul(dst[:, :], WG[:, k, P * e:P * (e + 1)], chan[:, k, :],
                                           start=(k == 0), stop=(k == DC - 1))
                ins.then_inc(S_["gate_mm"], 1)

            def low_rank(bk, bt):
                dst = bk.take(pe, ("lr", 0), bt=bt)
                pe.wait_ge(S_["um_done"], bt + 1)
                for k in range(DC):
                    ins = nc.tensor.matmul(dst[:, 0:RANK], umean[:, k:k + 1].broadcast_to([P, P]), lru[:, k, :],
                                           start=(k == 0), stop=(k == DC - 1))
                ins.then_inc(S_["lr_mm"], 1)

            def y_T(bk, r, s):
                dst = bk.take(pe, ("yT", s), r=r)
                pe.wait_ge(S_["yT_ok"], 4 * r + 4)
                for e in range(DC):
                    ins = nc.tensor.transpose(dst[:, P * e:P * (e + 1)], chan[:, e, P * s:P * (s + 1)], ident[:, :])
                ins.then_inc(S_["yT_mm"], 1)

            def h_T(bk, r, s):
                dst = bk.take(pe, ("hT2", s), r=r)
                pe.wait_ge(S_["p_norm"], 4 * r + s + 1)
                for c_ in range(DC):
                    ins = nc.tensor.transpose(dst[:, P * c_:P * (c_ + 1)], two[:, s % 2, P * c_:P * (c_ + 1)], ident[:, :])
                ins.then_inc(S_["hT2_mm"], 1)

            def piece(bk, p, n, bt):
                kind, s = p
                if kind == "xT":
                    attn_T(bk, n + TPB, s)
                elif kind == "gate":
                    gate(bk, n + TPB, s)
                elif kind == "lr":
                    low_rank(bk, bt + 1)
                elif kind == "yT":
                    y_T(bk, n + 1, s)
                else:
                    h_T(bk, n + 1, s)

            def project(dst, col, n, first, done):
                for k in range(DC):
                    if first:
                        pe.wait_ge(S_["x1_ok"], 4 * n + k + 1)
                    for w in (W1, W2):
                        nc.tensor.matmul(dst[:, :], w[:, k, col:col + P], X1[:, k, :],
                                         start=(k == 0 and w is W1), stop=False)
                for k in range(DC):
                    if first:
                        pe.wait_ge(S_["x2_ok"], 4 * n + k + 1)
                    ins = nc.tensor.matmul(dst[:, :], W1[:, k, col:col + P], X2[:, k, :],
                                           start=False, stop=(k == DC - 1))
                ins.then_inc(S_[done], 1)

            def down(n, i):
                q = NCH * n + i
                pe.wait_ge(S_["h1_ok"], q + 1)
                pe.wait_ge(S_["h2_ok"], START + q + 1)
                if i == 0:
                    pe.wait_ge(S_["y_used"], START + 4 * n)
                for s in range(NSUB):
                    sl = slice(P * s, P * (s + 1))
                    nc.tensor.matmul(yps[s][:, :], H1[:, i % 2, sl], V1[:, i, :], start=(i == 0), stop=False)
                    nc.tensor.matmul(yps[s][:, :], H1[:, i % 2, sl], V2[:, i, :], start=False, stop=False)
                    ins = nc.tensor.matmul(yps[s][:, :], H2[:, i % 2, sl], V1[:, i, :], start=False,
                                           stop=(i == NCH - 1))
                    if i == NCH - 1:
                        ins.then_inc(S_["y_mm"], 1)
                if i < NCH - 1:
                    ins.then_inc(S_["d_mm"], 1)

            pe.wait_ge(S_["ident_ok"], 2)
            pe.wait_ge(S_["silu_ok"], 1)
            for k in range(DC):
                ins = nc.tensor.transpose(bank[0][:, NB * k:NB * (k + 1)], csig[:, P * k:P * (k + 1)],
                                          ident[0:NB, 0:NB])
            ins.then_inc(S_["cT_mm"], 1)
            pe.wait_ge(S_["cT_ok"], 1)
            for k in range(DC):
                pe.wait_ge(wm_in[k % 2], 16 * (k // 2) + 16)
                for i in range(NMOD):
                    ins = nc.tensor.matmul(modps[i][0:NB, :], cT[:, k, :], wm[:, k % 2, D * i:D * (i + 1)],
                                           start=(k == 0), stop=(k == DC - 1))
                ins.then_inc(S_["mod_mm"], 1)
            pe.wait_ge(S_["mod_fix"], 2 * FIXES)
            for i in (SA, CA, GA, SB, CB):
                for c_ in range(DC):
                    src = mrow[:, D * i + P * c_:D * i + P * (c_ + 1)]
                    col = NB * (DC * i + c_)
                    ins = nc.tensor.transpose(bank[0][:, col:col + NB], src, ident[0:NB, 0:NB])
            ins.then_inc(S_["modt_mm"], 1)
            pe.wait_ge(S_["gw_in"], 16)
            for k in range(DC):
                if k == 0:
                    pe.wait_ge(S_["modt_ok"], 1)
                if k >= 2:
                    pe.wait_ge(S_["gw_ok"], k - 1)
                for e in range(DC):
                    ins = nc.tensor.transpose(bank[k % 2][:, P * e:P * (e + 1)], gwr[:, e, P * k:P * (k + 1)],
                                              ident[:, :])
                ins.then_inc(S_["gw_mm"], 1)
            pe.wait_ge(S_["gw_ok"], DC)
            pe.wait_ge(S_["lr_in"], 16 * (1 + DC))

            def dq(uu):
                gi, b0, nb_, kind, ch, col = UNITS[uu]
                if uu >= 6:
                    pe.wait_ge(S_["dq_raw"], uu - 5)
                pe.wait_ge(S_["dq_nib"], gi + 1)
                dst = dq_banks[uu % 6][:, :].bitcast(F16)
                for i, blk in enumerate(dq_blocks(uu)):
                    ins = nc.tensor.transpose(dst[:, P * i:P * (i + 1)], blk, ident16[:, :])
                ins.then_inc(S_["dq_mm"], 1)

            bk = Banks()
            for m in range(TPB):
                for s in range(NSUB):
                    attn_T(bk, m, s)
                for uu in DQ_AT[2 * m]:
                    dq(uu)
                for e in range(DC):
                    gate(bk, m, e)
                for uu in DQ_AT[2 * m + 1]:
                    dq(uu)
            low_rank(bk, 0)
            for kind, s in P_ORDER:
                (y_T if kind == "yT" else h_T)(bk, 0, s)
            pe.wait_ge(S_["dq_w2"], NU)

            SLOT = {1: [("xT", 0), ("xT", 1)], 2: [("xT", 2), ("xT", 3)], 3: [("gate", 0), ("gate", 1)],
                    4: [("gate", 2), ("gate", 3)], 5: [("lr", 0)],
                    7: [("yT", 0), ("yT", 1)], 8: [("yT", 2), ("hT2", 0)], 9: [("yT", 3), ("hT2", 1)],
                    10: [("hT2", 2), ("hT2", 3)]}

            def wanted(p, j, with_a, with_p):
                kind = p[0]
                if kind in ("xT", "gate"):
                    return with_a
                if kind == "lr":
                    return with_a and j == TPB - 1
                return with_p

            def step(bk, n, j, bt, with_a, with_p):
                for i in range(NCH):
                    q = NCH * n + i
                    pe.wait_ge(S_["gs_ok"], START + q)
                    project(gps, P * i, n, i == 0, "g_mm")
                    pe.wait_ge(S_["h_ok"], START + q)
                    project(ups, HID + P * i, n, i == 0, "u_mm")
                    ps = [p for p in SLOT.get(i, []) if wanted(p, j, with_a, with_p)]
                    for p in ps[:1]:
                        piece(bk, p, n, bt)
                    if i:
                        down(n, i - 1)
                    for p in ps[1:]:
                        piece(bk, p, n, bt)
                down(n, NCH - 1)

            with pe.Fori(0, NB - 1) as bt:
                bk.hist = [(("hT2", 2), None, TPB * bt, None), (("hT2", 3), None, TPB * bt, None)]
                for j in range(TPB):
                    step(bk, TPB * bt + j, j, bt, True, True)
            bk = Banks()
            bk.hist = [(("hT2", 2), None, TPB * (NB - 1), None), (("hT2", 3), None, TPB * (NB - 1), None)]
            for j in range(TPB):
                step(bk, TPB * (NB - 1) + j, j, NB - 1, False, j < TPB - 1)


_INS = ['L0_attn_u', 'L0_attn_a', 'L0_attn_b', 'L0_attn_c', 'L0_attn_d', 'L0_attn_gate_w', 'L0_attn_gate_b',
        'L0_attn_d_lr_u', 'L0_attn_d_lr_v', 'L0_ffn_gate_up_packed', 'L0_ffn_gate_up_scales',
        'L0_ffn_down_packed', 'L0_ffn_down_scales', 'L0_c', 'L0_wmod']


def kernel(**inputs):
    import numpy as _np
    import concourse.bacc as _bacc
    from concourse import mybir as _mybir
    from concourse.bass_utils import run_bass_kernel_spmd as _run

    nc = _bacc.Bacc("TRN2", target_bir_lowering=False, num_devices=1)
    arrays, args = {}, []
    for name in _INS:
        a = _np.ascontiguousarray(inputs[name])
        arrays[f"in_{name}_dram"] = a
        args.append(nc.dram_tensor(f"in_{name}_dram", a.shape, _mybir.dt.from_np(a.dtype), kind="ExternalInput").ap())
    shape = tuple(inputs['L0_attn_u'].shape)
    args.append(nc.dram_tensor("out_0_dram", shape, _mybir.dt.from_np(_np.dtype('float32')), kind="ExternalOutput").ap())
    adaln_block_kernel(nc, *args)
    r = _run(nc, [arrays], core_ids=[0])
    return r.results[0]["out_0_dram"]
```

```python
import numpy as np
import concourse.bass as bass
from concourse import mybir
from contextlib import ExitStack

F32 = mybir.dt.float32
F32R = mybir.dt.float32r
F16 = mybir.dt.float16
I32 = mybir.dt.int32
ALU = mybir.AluOpType
ACT = mybir.ActivationFunctionType

P = 128


def adaln_block_kernel(nc, u, a, b, c, d, gate_w, gate_b, d_lr_u, d_lr_v,
                       gu_packed, gu_scales, dn_packed, dn_scales, cond, wmod, out):
    NB, T, D = u.shape
    HID = gu_packed.shape[0] // 2
    RANK = d_lr_u.shape[1]
    NMOD = wmod.shape[1] // D
    TOK = 512
    NSUB = TOK // P
    TPB = T // TOK
    DC = D // P
    NCH = HID // P
    WPG = P // 8
    SHIFT_UP = 2.0 ** 14
    LN_EPS = 1e-5
    RMS_EPS = 1e-6
    SA, CA, GA, SB, CB, GB = range(6)

    xv = u.rearrange("b (j s p) d -> (b j) s p d", p=P, s=NSUB)
    ov = out.rearrange("b (j s p) d -> (b j) s p d", p=P, s=NSUB)

    ug_dram = nc.dram_tensor("ug_scratch", [NB * TPB, P, DC, TOK], F32).ap()
    xn_dram = nc.dram_tensor("xnew_scratch", [NB * TPB, NSUB, P, D], F32).ap()
    gb_dram = nc.dram_tensor("gb_scratch", [NB, D], F32).ap()

    with ExitStack() as ctx:
        def sb(name, shape, dt, scope=ctx):
            return scope.enter_context(nc.sbuf_tensor(name, shape, dt))

        def pb(name):
            return ctx.enter_context(nc.psum_tensor(name, [P, 512], F32))

        def sem(name):
            return ctx.enter_context(nc.semaphore(name))

        W1 = sb("gu_w1", [P, DC, 2 * HID], F32R)
        W2 = sb("gu_w2", [P, DC, 2 * HID], F32R)
        WG = sb("gate_wT", [P, DC, D], F32)
        chan = sb("chan", [P, DC, TOK], F32)
        xa = sb("xa", [P, 2, D], F32)
        xb = sb("xb", [P, 2, D], F32)
        two = sb("two", [P, 2, D], F32)
        ugo = sb("ugo", [P, 2, TOK], F32)
        ident = sb("ident", [P, P], F32)
        vec = sb("vec", [P, 5, DC], F32)
        modT = sb("modT", [P, NB, 5, DC], F32)
        modA = sb("modA", [P, 2, DC], F32)
        modP = sb("modP", [P, 2, DC], F32)
        coef = sb("coef", [P, 2, DC], F32)
        usum = sb("usum", [P, DC, TPB], F32)
        umean = sb("umean", [P, DC], F32)
        lru = sb("lru", [P, DC, RANK], F32)
        lrv = sb("lrv", [P, DC, RANK], F32)
        lrp = sb("lrp", [P, DC, RANK], F32)
        carry = sb("carry", [P, DC], F32)
        stat = sb("stat", [P, 4, 6], F32)
        mvA = sb("mvA", [P, 2, 2], F32)
        mvP = sb("mvP", [P, 2, 2], F32)
        rsA = sb("rsA", [P, 2, 2], F32)
        rsP = sb("rsP", [P, 2, 2], F32)
        ssq = sb("ssq", [P, NSUB], F32)
        rms = sb("rms", [P, NSUB, 2], F32)
        consts = sb("consts", [P, 3], F32)
        k_pow = consts[:, 0:1]
        k_eps = consts[:, 1:3]
        vecs = sb("vecs", [P, 5, DC], F32)
        aa = vecs[:, 0, :]
        f0 = vecs[:, 1, :]
        bc_ = vecs[:, 2, :]
        dlr = vecs[:, 3, :]
        deff = vecs[:, 4, :]
        cT = sb("cT", [P, DC, NB], F32)
        crow, csig = xb[0:NB, 0, :], xb[0:NB, 1, :]
        gwr = chan

        with ExitStack() as early:
            wm = sb("wm", [P, 2, DC, D], F32, early)
            mrow = sb("mrow", [NB, NMOD * D], F32, early)
            mtmp = sb("mtmp", [NB, D], F32, early)
            chan_b = sb("chan_b", [P, DC, TOK], F32, early)
            xa_b = sb("xa_b", [P, 2, D], F32, early)
        V1 = sb("dn_w1", [P, NCH, D], F32R)
        V2 = sb("dn_w2", [P, NCH, D], F32R)
        with ExitStack() as early:
            gpk = sb("gu_words", [P, 2 * NCH, D // 8], I32, early)
            dpk = sb("dn_words", [P, DC, HID // 8], I32, early)
            scl = sb("scales", [P, 2, 2 * HID], F16, early)
            raw = sb("raw", [P, 2, 512], F32, early)
            nib = sb("nib", [P, 2 * HID], I32, early)
            ident16 = sb("ident16", [P, P], F16, early)
        X1 = sb("ffn_x1", [P, DC, TOK], F32R)
        X2 = sb("ffn_x2", [P, DC, TOK], F32R)
        S = sb("silu_up", [P, 2, TOK], F32)
        H1 = sb("h1", [P, 2, TOK], F32R)
        H2 = sb("h2", [P, 2, TOK], F32R)
        ysc = sb("y_scaled", [P, 2, D], F32)
        gbB = sb("gb_rows", [P, D], F32)
        yo = [ugo[:, 0, :], ugo[:, 1, :], ysc[:, 0, :], ysc[:, 1, :]]
        fin = [xb[:, 0, :], xb[:, 1, :], two[:, 0, :], two[:, 1, :]]

        bank = [pb("bank0"), pb("bank1")]
        gps = pb("gate_ps")
        ups = pb("up_ps")
        yps = [pb(f"y_ps{s}") for s in range(NSUB)]
        dq_banks = [ups] + yps[0:2]
        xT_banks = yps[2:4]
        NDQ = len(dq_banks)
        modps = gps

        S_ = {n: sem(n) for n in """
            cond_in vec_in lr_in gw_in gpk_in dpk_in ident_ok const_ok
            csig_ok silu_ok cT_mm cT_ok mod_mm mod_row modt_mm modt_ok mod_fix gb_saved
            gw_mm gw_ok gw_dve vec_tanh vec_fix
            dq_mm dq_top dq_nib dq_raw dq_w1 dq_w2
            a_stat a_mv a_eps a_rstd a_norm xT_mm hT_ok modA_ok gate_mm gate_sig ug_done
            um_done lr_mm lr_prod lr_sum d_eff d_tmp coef_ok
            p_first p_scan carry_ok p_mul yT_ok yT_mm x_new p_stat p_mv p_eps p_rstd p_norm hT2_mm modP_ok x_next
            x1_ok x2_ok g_mm u_mm sig_ok gs_ok h_ok h1_ok h2_ok d_mm
            y_mm sq_ok rms_a rms_ok y_used out_ok gb_in
        """.split()}
        wm_in = [sem(f"wm_in{i}") for i in range(2)]
        scl_in = [sem(f"scl_in{i}") for i in range(2)]
        xa_in = [sem(f"xa_in{i}") for i in range(2)]
        xab_in = [sem(f"xab_in{i}") for i in range(2)]
        xb_in = [sem(f"xb_in{i}") for i in range(2)]
        fin_in = [sem(f"fin_in{i}") for i in range(NSUB)]
        ug_out = [sem(f"ug_out{i}") for i in range(2)]
        ug_in = sem("ug_in")
        xn_out = [sem(f"xn_out{i}") for i in range(2)]
        y_out = [sem(f"y_out{i}") for i in range(NSUB)]

        START = 1
        STARTED = {"dve": [S_[k] for k in ("gs_ok", "h_ok", "y_used")],
                   "pool": [S_[k] for k in ("out_ok", "h2_ok")],
                   "pe": [S_[k] for k in ("y_mm", "d_mm")], "sp": y_out, "act": [S_["sq_ok"]]}

        def early_tile(m):
            return isinstance(m, int) and m < TPB

        def rows_of(m, s):
            return (xa_b if early_tile(m) and s >= 2 else xa)[:, s % 2, :]

        def hT_of(m):
            return chan_b if early_tile(m) and m % 2 == 0 else chan

        def rows_in(eng, m, s):
            if early_tile(m):
                eng.wait_ge((xab_in if s >= 2 else xa_in)[s % 2], 16 * m + 16)
            else:
                eng.wait_ge(xa_in[s % 2], 32 * m - 16 * TPB + 16 * (s // 2) + 16)

        GROUPS = [("gu", g, 1) for g in range(DC)] + [("dn", c_, min(4, NCH - c_)) for c_ in range(0, NCH, 4)]
        FIXES = 4
        UNITS = []
        for gi, (kind, c0, nc_) in enumerate(GROUPS):
            if kind == "gu":
                UNITS += [(gi, o, min(4, 2 * NCH - o), kind, c0, P * o) for o in range(0, 2 * NCH, 4)]
            else:
                UNITS += [(gi, c_, DC, kind, c0 + c_, 0) for c_ in range(nc_)]
        NU = len(UNITS)
        GROUP_END = [sum(1 for x in UNITS if x[0] <= gi) for gi in range(len(GROUPS))]

        def dq_blocks(uu):
            gi, b0, nb_, kind, ch, col = UNITS[uu]
            n_ = GROUPS[gi][2]
            v = nib[:, :].bitcast(F16)
            for i in range(nb_):
                blk = b0 + i if kind == "gu" else i * n_ + b0
                yield v[:, 2 * P * blk + 1:2 * P * (blk + 1):2]

        def dq_dst(uu, which):
            gi, b0, nb_, kind, ch, col = UNITS[uu]
            w = (W1, W2) if kind == "gu" else (V1, V2)
            return w[which][:, ch, col:col + P * nb_]

        MODS = [CA, SA, GA, GB, CB, SB]
        PROLOGUE = []
        todo = list(range(NU))

        def some(n_, may_unpack=True):
            steps = []
            while todo and len(steps) < n_:
                first = todo[0] == 0 or UNITS[todo[0]][0] != UNITS[todo[0] - 1][0]
                if first and ("unpack", UNITS[todo[0]][0]) not in PROLOGUE + steps:
                    if not may_unpack:
                        break
                    steps.append(("unpack", UNITS[todo[0]][0]))
                else:
                    steps.append(("dq", todo.pop(0)))
            return steps

        MOD_STEPS = {0: [("mod", 2)], 1: [("fix", 2), ("modT", 2)], 2: [("mod", 3)], 3: [("fix", 3), ("mod", 4)],
                     4: [("modT", 4), ("mod", 5)], 5: [("modT", 5)]}
        PROLOGUE += [("xT", 0, s) for s in range(NSUB)] + [("norm", 1, 0)]
        for m in range(TPB):
            for e in range(DC):
                if m + 1 < TPB:
                    PROLOGUE += [("xT", m + 1, e)]
                PROLOGUE += some(1)
                if e == 0 and m + 1 < TPB:
                    PROLOGUE += [("norm", m + 1, 1)]
                if e == DC - 1 and m + 2 < TPB:
                    PROLOGUE += [("norm", m + 2, 0)]
                PROLOGUE += [("gate", m, e)] + MOD_STEPS.get(DC * m + e, [])
                PROLOGUE += some(1, may_unpack=False)
        PROLOGUE += [("sum", 0)] + some(2) + [("deff", 0)]
        for e in range(DC):
            PROLOGUE += [("scan", e)] + some(1)
        PROLOGUE += [("yT", 0), ("yT", 1), ("yT", 2), ("hT2", 0), ("yT", 3), ("hT2", 1)] + some(1)
        PROLOGUE += [("hT2", 2), ("hT2", 3)] + some(NU)

        MOD_T = [0, 1] + [x[1] for x in PROLOGUE if x[0] == "modT"]

        A_ORDER = [("xT", 0), ("xT", 1), ("xT", 2), ("xT", 3), ("gate", 0), ("gate", 1), ("gate", 2), ("gate", 3)]
        P_ORDER = [("yT", 0), ("yT", 1), ("yT", 2), ("hT2", 0), ("yT", 3), ("hT2", 1), ("hT2", 2), ("hT2", 3)]

        def freed(eng, piece, m, r, bt):
            kind, s = piece
            if kind == "xT":
                eng.wait_ge(S_["hT_ok"], 4 * m + s + 1)
            elif kind == "gate":
                eng.wait_ge(S_["gate_sig"], 4 * m + s + 1)
            elif kind == "lr":
                eng.wait_ge(S_["lr_prod"], bt + 1)
            elif kind == "yT":
                eng.wait_ge(S_["x_new"], 4 * r + s + 1)
            else:
                eng.wait_ge(S_["x_next"], 4 * r + s + 1)

        class Banks:
            def __init__(self, banks=bank):
                self.hist, self.banks = [], banks

            def take(self, eng, piece, m=None, r=None, bt=None):
                if len(self.hist) >= 2:
                    freed(eng, *self.hist[-2])
                if piece[0] == "lr":
                    self.hist[-2] = (piece, m, r, bt)
                    return self.banks[0]
                self.hist.append((piece, m, r, bt))
                return self.banks[(len(self.hist) - 1) % 2]

        def bank_of(piece, j, with_a):
            order = {"xT": A_ORDER, "gate": A_ORDER, "lr": [piece]}.get(piece[0], P_ORDER)
            return bank[order.index(piece) % 2]

        block = ctx.enter_context(nc.Block())

        @block.sync
        def _(sp):
            for first in STARTED["sp"]:
                sp.sem_inc(first, START)
            wmv = wmod.rearrange("(k p) (i d) -> i p k d", p=P, d=D)

            def load_mod(t):
                if t >= 2:
                    sp.wait_ge(S_["mod_mm"], t - 1)
                sp.dma_start(wm[:, t % 2, :, :], wmv[MODS[t]]).then_inc(wm_in[t % 2], 16)

            def load_scales(gi):
                kind, c0, n_ = GROUPS[gi]
                if gi >= 2:
                    sp.wait_ge(S_["dq_raw"], GROUP_END[gi - 2])
                if kind == "gu":
                    src, size = gu_scales[c0:c0 + 1, :], 2 * HID
                else:
                    src, size = dn_scales[c0:c0 + n_, :].rearrange("g o -> (g o)").unsqueeze(0), n_ * D
                sp.dma_start(scl[:, gi % 2, 0:size], src.broadcast_to([P, size])).then_inc(scl_in[gi % 2], 16)

            def load_x_attn(m, s):
                if early_tile(m):
                    if m:
                        sp.wait_ge(S_["xT_mm"], 4 * m + s - 3)
                    arrived = xab_in if s >= 2 else xa_in
                else:
                    sp.wait_ge(S_["xT_mm"], 4 * m + s - 1)
                    arrived = xa_in
                sp.dma_start(rows_of(m, s), xv[m, s, :, :]).then_inc(arrived[s % 2], 16)

            sp.dma_start(crow, cond).then_inc(S_["cond_in"], 16)
            load_mod(0)
            load_mod(1)
            for s in range(NSUB):
                load_x_attn(0, s)
            sp.dma_start(gwr[:, :, :], gate_w.rearrange("(c p) d -> p c d", p=P)).then_inc(S_["gw_in"], 16)
            gsrc = gu_packed.rearrange("(c w j) k -> j w c k", w=WPG, j=8)
            for j in range(8):
                sp.dma_start(gpk[WPG * j:WPG * (j + 1), :, :], gsrc[j]).then_inc(S_["gpk_in"], 16)
            load_scales(0)
            with nc.allow_non_contiguous_dma(reason="small vectors by channel"):
                for i, v in enumerate((a, b, c, d, gate_b)):
                    sp.dma_start(vec[:, i, :], v.rearrange("(c p) -> p c", p=P)).then_inc(S_["vec_in"], 16)
                for c_ in range(DC):
                    sp.dma_start(lrv[:, c_, :], d_lr_v[:, P * c_:P * (c_ + 1)].rearrange("r p -> p r")
                                 ).then_inc(S_["lr_in"], 16)
            load_scales(1)
            load_mod(2)
            sp.dma_start(lru[:, :, :], d_lr_u.rearrange("(c p) r -> p c r", p=P)).then_inc(S_["lr_in"], 16)
            sp.dma_start(dpk[:, :, :], dn_packed.rearrange("(c p) k -> p c k", p=P)).then_inc(S_["dpk_in"], 16)

            def store_ug(m, e):
                sp.wait_ge(S_["ug_done"], 4 * m + e + 1)
                sp.dma_start(ug_dram[m, :, e, :], ugo[:, e % 2, :]).then_inc(ug_out[e % 2], 16)

            def load_ug(r, m):
                if m is not None:
                    sp.wait_ge(S_["ug_done"], 4 * m + 4)
                else:
                    sp.wait_ge(S_["x2_ok"], 4 * r)
                for k in range(2):
                    sp.wait_ge(ug_out[k], 32 * r + 32)
                sp.dma_start(chan[:, :, :], ug_dram[r, :, :, :]).then_inc(ug_in, 16)

            def load_x_prep(r, s, first):
                if s < 2:
                    if not first:
                        sp.wait_ge(S_["p_norm"], 4 * r)
                        sp.wait_ge(y_out[s], START + 16 * r - 16)
                        sp.wait_ge(xn_out[s % 2], 32 * r)
                else:
                    sp.wait_ge(xn_out[s % 2], 32 * r + 16)
                    sp.wait_ge(S_["p_norm"], 4 * r + s - 1)
                sp.dma_start(xb[:, s % 2, :], xv[r, s, :, :]).then_inc(xb_in[s % 2], 16)

            def store_x_new(r, s):
                sp.wait_ge(S_["x_new"], 4 * r + s + 1)
                sp.dma_start(xn_dram[r, s, :, :], xb[:, s % 2, :]).then_inc(xn_out[s % 2], 16)

            def load_x_final(n, s, r):
                if r is not None and s < 2:
                    sp.wait_ge(S_["p_norm"], 4 * r + s + 3)
                    sp.wait_ge(xn_out[s % 2], 32 * r + 32)
                elif r is not None:
                    sp.wait_ge(S_["hT2_mm"], 4 * r + s + 1)
                else:
                    sp.wait_ge(y_out[s], START + 16 * n)
                    sp.wait_ge(xn_out[s % 2], 32 * n + 32)
                sp.dma_start(fin[s], xn_dram[n, s, :, :]).then_inc(fin_in[s], 16)

            def store_out(n, s):
                sp.wait_ge(S_["out_ok"], START + 4 * n + s + 1)
                sp.dma_start(ov[n, s, :, :], fin[s]).then_inc(y_out[s], 16)

            def prep(r, m, first=False):
                load_ug(r, m)
                load_x_prep(r, 0, first)
                load_x_prep(r, 1, first)
                for s in range(NSUB):
                    store_x_new(r, s)
                    if s < 2:
                        load_x_prep(r, s + 2, first)

            for item in PROLOGUE:
                kind, q = item[0], item[1]
                if kind == "xT" and q < TPB - 1:
                    load_x_attn(q + 1, item[2])
                if kind == "mod" and q < NMOD - 1:
                    load_mod(q + 1)
                if kind == "modT" and q == 4:
                    sp.wait_ge(S_["mod_fix"], 2 * FIXES)
                    sp.dma_start(gb_dram, mrow[:, GB * D:(GB + 1) * D]).then_inc(S_["gb_saved"], 16)
                if kind == "gate":
                    store_ug(q, item[2])
                if kind == "dq" and UNITS[q][1] == 0 and UNITS[q][0] + 1 < len(GROUPS) and UNITS[q][0] >= 1:
                    load_scales(UNITS[q][0] + 1)
                if kind == "sum":
                    load_x_prep(0, 0, True)
                    load_x_prep(0, 1, True)
                    load_ug(0, TPB - 1)
            for s in range(NSUB):
                store_x_new(0, s)
                if s < 2:
                    load_x_prep(0, s + 2, True)

            def step(n, j, with_a, with_p):
                m, r = n + TPB, n + 1
                if j == 0:
                    if not isinstance(n, int) or n > 0:
                        sp.wait_ge(S_["out_ok"], START + 4 * n)
                    sp.wait_ge(S_["dq_w2"], NU)
                    sp.wait_ge(S_["gb_saved"], 16)
                    bt = n // TPB if isinstance(n, int) else (n_batch[0])
                    sp.dma_start(gbB[:, :], gb_dram[bt:bt + 1, :].broadcast_to([P, D]) if isinstance(bt, int)
                                 else gb_dram[bass.ds(bt, 1), :].broadcast_to([P, D])).then_inc(S_["gb_in"], 16)
                if with_a:
                    for s in range(NSUB):
                        load_x_attn(m, s)
                        if s == 1 and j:
                            for s_out in range(NSUB):
                                store_out(n - 1, s_out)
                    for e in range(DC):
                        store_ug(m, e)
                if with_p:
                    prep(r, m if with_a else None, first=False)
                for s in range(NSUB):
                    load_x_final(n, s, r if with_p else None)
                if not with_a or j == TPB - 1:
                    for s in range(NSUB):
                        store_out(n, s)

            n_batch = [None]
            with sp.Fori(0, NB - 1) as bt:
                n_batch[0] = bt
                for j in range(TPB):
                    step(TPB * bt + j, j, True, True)
            for j in range(TPB):
                step(TPB * (NB - 1) + j, j, False, j < TPB - 1)
            for s in range(NSUB):
                sp.wait_ge(y_out[s], START + 16 * NB * TPB)
            sp.wait_ge(S_["gb_saved"], 16)
            for k in range(2):
                sp.wait_ge(xn_out[k], 32 * NB * TPB)
                sp.wait_ge(ug_out[k], 32 * NB * TPB)

        @block.gpsimd
        def _(pool):
            for first in STARTED["pool"]:
                pool.sem_inc(first, START)
            nc.gpsimd.memset(ident[:, :], 0.0).then_inc(S_["const_ok"], 1)
            nc.gpsimd.memset(k_pow[:, :], -0.5).then_inc(S_["const_ok"], 1)
            nc.gpsimd.memset(k_eps[:, 0:1], LN_EPS).then_inc(S_["const_ok"], 1)
            nc.gpsimd.memset(k_eps[:, 1:2], RMS_EPS * SHIFT_UP ** -2).then_inc(S_["const_ok"], 1)
            pool.wait_ge(S_["const_ok"], 4)
            nc.gpsimd.affine_select(out=ident[:, :], in_=ident[:, :], compare_op=ALU.not_equal, fill=1.0,
                                    base=0, pattern=[[-1, P]], channel_multiplier=1).then_inc(S_["ident_ok"], 1)
            pool.wait_ge(S_["ident_ok"], 1)
            nc.gpsimd.tensor_copy(ident16[:, :], ident[:, :]).then_inc(S_["ident_ok"], 1)

            def rstd(mv, rs, s, got, mid, done, idx):
                pool.wait_ge(S_[got], idx + 1)
                nc.gpsimd.tensor_tensor(rs[:, s % 2, 0:1], mv[:, s % 2, 1:2], k_eps[:, 0:1],
                                        ALU.add).then_inc(S_[mid], 1)
                pool.wait_ge(S_[mid], idx + 1)
                nc.gpsimd.tensor_tensor(rs[:, s % 2, 1:2], rs[:, s % 2, 0:1], k_pow[:, :],
                                        ALU.pow).then_inc(S_[done], 1)

            def rstd_a(m, s):
                rstd(mvA, rsA, s, "a_mv", "a_eps", "a_rstd", 4 * m + s)

            def rstd_p(r, s):
                rstd(mvP, rsP, s, "p_mv", "p_eps", "p_rstd", 4 * r + s)

            def final(n):
                for s in range(NSUB):
                    pool.wait_ge(S_["sq_ok"], START + 4 * n + s + 1)
                    nc.gpsimd.tensor_tensor(rms[:, s, 0:1], ssq[:, s:s + 1], k_eps[:, 1:2],
                                            ALU.add).then_inc(S_["rms_a"], 1)
                    pool.wait_ge(S_["rms_a"], 4 * n + s + 1)
                    nc.gpsimd.tensor_tensor(rms[:, s, 1:2], rms[:, s, 0:1], k_pow[:, :],
                                            ALU.pow).then_inc(S_["rms_ok"], 1)

            def dq_low(uu):
                pool.wait_ge(S_["dq_w1"], uu + 1)
                nc.gpsimd.tensor_tensor(dq_dst(uu, 1), raw[:, uu % 2, 0:P * UNITS[uu][2]], dq_dst(uu, 0).bitcast(F32),
                                        ALU.subtract).then_inc(S_["dq_w2"], 1)

            def chunk_h2(n, i):
                q = NCH * n + i
                pool.wait_ge(S_["h1_ok"], q + 1)
                nc.gpsimd.tensor_tensor(H2[:, i % 2, :], S[:, i % 2, :], H1[:, i % 2, :].bitcast(F32),
                                        ALU.subtract).then_inc(S_["h2_ok"], 1)

            for s in range(NSUB):
                rstd_a(0, s)
            for item in PROLOGUE:
                kind, q = item[0], item[1]
                if kind == "norm":
                    rstd_a(q, 2 * item[2])
                    rstd_a(q, 2 * item[2] + 1)
                if kind == "dq":
                    dq_low(q)
                if kind == "yT":
                    rstd_p(0, q)

            def step(n, j, with_a, with_p):
                for i in range(NCH):
                    if with_a and i in (0, 1):
                        rstd_a(n + TPB, 2 * i)
                        rstd_a(n + TPB, 2 * i + 1)
                    chunk_h2(n, i)
                    if with_a and i == 0 and j:
                        add_out(n - 1, NSUB - 1)
                    if with_p:
                        for s in {7: (0, 1), 8: (2,), 9: (3,)}.get(i, ()):
                            rstd_p(n + 1, s)
                final(n)
                for s in range(NSUB if not with_a or j == TPB - 1 else NSUB - 1):
                    add_out(n, s)

            def add_out(n, s):
                pool.wait_ge(fin_in[s], 16 * n + 16)
                pool.wait_ge(S_["y_used"], START + 4 * n + s + 1)
                nc.gpsimd.tensor_tensor(fin[s], yo[s], fin[s], ALU.add).then_inc(S_["out_ok"], 1)

            with pool.Fori(0, NB - 1) as bt:
                for j in range(TPB):
                    step(TPB * bt + j, j, True, True)
            for j in range(TPB):
                step(TPB * (NB - 1) + j, j, False, j < TPB - 1)

        @block.scalar
        def _(act):
            for first in STARTED["act"]:
                act.sem_inc(first, START)
            def batch_cols(dst, rows, bt, done):
                for i, row in enumerate(rows):
                    src = modT[:, bass.ds(bt, 1), row, :] if not isinstance(bt, int) else modT[:, bt:bt + 1, row, :]
                    ins = nc.scalar.activation(dst[:, i:i + 1, :], src, ACT.Copy)
                ins.then_inc(S_[done], 1)
                act.wait_ge(S_[done], bt + 1)

            def x_evac(m, s, j, first_piece_wait):
                if j == 0 and s == 0:
                    batch_cols(modA, (SA, CA), bt_of(m), "modA_ok")
                act.wait_ge(S_["xT_mm"], 4 * m + s + 1)
                if s == 0 and first_piece_wait is not None:
                    act.wait_ge(S_["x2_ok"], first_piece_wait)
                if s == 0 and early_tile(m) and m >= 2:
                    act.wait_ge(S_["ug_done"], 4 * m - 4)
                src = xT_banks[s % 2] if early_tile(m) else bank_of(("xT", s), j, True)
                for c_ in range(DC):
                    ins = nc.scalar.activation(hT_of(m)[:, c_, P * s:P * (s + 1)], src[:, P * c_:P * (c_ + 1)],
                                               ACT.Identity, bias=modA[:, 0, c_:c_ + 1], scale=modA[:, 1, c_:c_ + 1])
                ins.then_inc(S_["hT_ok"], 1)

            def gate_sig(m, e):
                act.wait_ge(S_["gate_mm"], 4 * m + e + 1)
                if e < 2:
                    if isinstance(m, int):
                        if m:
                            act.wait_ge(S_["ug_done"], 4 * m + e - 1)
                    else:
                        act.wait_ge(y_out[2 + e], START + 16 * (m - TPB))
                        act.wait_ge(S_["hT2_mm"], 4 * (m - TPB) + 4)
                else:
                    act.wait_ge(S_["ug_done"], 4 * m + e - 1)
                nc.scalar.activation(two[:, e % 2, :], bank_of(("gate", e), 0, True)[:, :], ACT.Sigmoid,
                                     bias=vec[:, 4, e:e + 1]).then_inc(S_["gate_sig"], 1)

            def h_evac(r, s, j_r, ffn_before):
                if j_r == 0 and s == 0:
                    batch_cols(modP, (SB, CB), bt_of(r), "modP_ok")
                act.wait_ge(S_["hT2_mm"], 4 * r + s + 1)
                src = bank_of(("hT2", s), 0, True)
                for c_ in range(DC):
                    ins = nc.scalar.activation(chan[:, c_, P * s:P * (s + 1)], src[:, P * c_:P * (c_ + 1)],
                                               ACT.Identity, bias=modP[:, 0, c_:c_ + 1], scale=modP[:, 1, c_:c_ + 1])
                ins.then_inc(S_["x_next"], 1)

            def split_x(r, c_, ffn_before):
                if c_ == 0:
                    act.wait_ge(S_["x_next"], 4 * r + 4)
                    if ffn_before:
                        act.wait_ge(S_["u_mm"], NCH * r)
                nc.scalar.activation(X1[:, c_, :], chan[:, c_, :], ACT.Copy).then_inc(S_["x1_ok"], 1)

            def chunk_sig(n, i):
                q = NCH * n + i
                act.wait_ge(S_["g_mm"], q + 1)
                act.wait_ge(S_["h2_ok"], START + (q - 1 if i else q))
                if i == 1:
                    act.wait_ge(S_["sq_ok"], START + 4 * n)
                nc.scalar.activation(S[:, i % 2, :], gps[:, :], ACT.Sigmoid, scale=SHIFT_UP).then_inc(S_["sig_ok"], 1)

            def chunk_h1(n, i):
                q = NCH * n + i
                act.wait_ge(S_["h_ok"], START + q + 1)
                if i == 0:
                    act.wait_ge(S_["y_mm"], START + 4 * n)
                else:
                    act.wait_ge(S_["d_mm"], START + (NCH - 1) * n + i - 1)
                nc.scalar.activation(H1[:, i % 2, :], S[:, i % 2, :], ACT.Copy).then_inc(S_["h1_ok"], 1)

            def final(n):
                act.wait_ge(S_["h2_ok"], START + NCH * n + NCH - 1)
                for s in range(NSUB):
                    act.wait_ge(S_["y_mm"], START + 4 * n + s + 1)
                    if s:
                        act.wait_ge(S_["sq_ok"], START + 4 * n + s)
                    nc.scalar.activation(S[:, 1, :], yps[s][:, :], ACT.Square, scale=float(D) ** -0.5,
                                         accum_out=ssq[:, s:s + 1]).then_inc(S_["sq_ok"], 1)

            cur = {}

            def bt_of(t):
                return t // TPB if isinstance(t, int) else cur["bt"] + 1

            act.wait_ge(S_["cond_in"], 16)
            nc.scalar.activation(csig, crow, ACT.Sigmoid).then_inc(S_["csig_ok"], 1)
            act.wait_ge(S_["cT_mm"], 1)
            nc.scalar.activation(cT[:, :, :], bank[0][:, 0:DC * NB].rearrange("p (c b) -> p c b", b=NB),
                                 ACT.Copy).then_inc(S_["cT_ok"], 1)

            def mod(t):
                i = MODS[t]
                act.wait_ge(S_["mod_mm"], t + 1)
                dst, src = mrow[:, D * i:D * (i + 1)], modps[0:NB, :]
                if i in (SB, CB):
                    dst = dst.rearrange("b (c j w) -> b c w j", j=8, w=WPG)
                    src = src.rearrange("b (c w j) -> b c w j", j=8, w=WPG)
                nc.scalar.activation(dst, src, ACT.Identity,
                                     bias=1.0 if i in (CA, CB) else 0.0).then_inc(S_["mod_row"], 1)

            def mod_T(t):
                act.wait_ge(S_["modt_mm"], MOD_T.index(t) + 1)
                nc.scalar.activation(modT[:, :, MODS[t], :],
                                     modps[:, 0:DC * NB].rearrange("p (c b) -> p b c", b=NB),
                                     ACT.Copy).then_inc(S_["modt_ok"], 1)

            def dq(uu):
                if uu == GROUP_END[DC - 1]:
                    act.wait_ge(S_["gb_saved"], 16)
                    act.wait_ge(S_["ug_done"], 4 * (TPB - 1))
                    act.wait_ge(S_["xT_mm"], 4 * TPB)
                act.wait_ge(S_["dq_raw"], uu + 1)
                nc.scalar.activation(dq_dst(uu, 0), raw[:, uu % 2, 0:P * UNITS[uu][2]],
                                     ACT.Copy).then_inc(S_["dq_w1"], 1)

            mod(0)
            mod_T(0)
            mod(1)
            mod_T(1)
            for k in range(DC):
                act.wait_ge(S_["gw_mm"], k + 1)
                nc.scalar.activation(WG[:, k, :], bank[k % 2][:, :], ACT.Copy).then_inc(S_["gw_ok"], 1)
            act.wait_ge(S_["vec_in"], 80)
            nc.scalar.activation(aa[:, :], vec[:, 0, :], ACT.Tanh).then_inc(S_["vec_tanh"], 1)
            act.wait_ge(S_["modt_ok"], 2)
            for item in PROLOGUE:
                kind, q = item[0], item[1]
                if kind == "xT":
                    x_evac(q, item[2], q, None)
                elif kind == "gate":
                    gate_sig(q, item[2])
                elif kind == "dq":
                    dq(q)
                elif kind == "mod":
                    mod(q)
                elif kind == "modT":
                    mod_T(q)
                elif kind == "hT2":
                    if q == 0:
                        act.wait_ge(S_["modt_ok"], len(MOD_T))
                    h_evac(0, q, 0, False)
            act.wait_ge(S_["dq_w2"], NU)
            for c_ in range(DC):
                split_x(0, c_, False)

            def step(n, j, with_a, with_p):
                m, r = n + TPB, n + 1
                for i in range(NCH):
                    chunk_sig(n, i)
                    chunk_h1(n, i)
                    if with_a:
                        if i in (1, 2):
                            for s in (2 * i - 2, 2 * i - 1):
                                x_evac(m, s, j, 4 * n + 4)
                        if i in (3, 4):
                            for e in (2 * i - 6, 2 * i - 5):
                                gate_sig(m, e)
                    if with_p:
                        for s in {8: (0,), 9: (1,), 10: (2, 3)}.get(i, ()):
                            h_evac(r, s, (j + 1) % TPB, True)
                if with_p:
                    for c_ in range(DC):
                        split_x(r, c_, True)
                final(n)

            with act.Fori(0, NB - 1) as bt:
                cur["bt"] = bt
                for j in range(TPB):
                    step(TPB * bt + j, j, True, True)
            for j in range(TPB):
                step(TPB * (NB - 1) + j, j, False, j < TPB - 1)

        @block.vector
        def _(dve):
            for first in STARTED["dve"]:
                dve.sem_inc(first, START)

            def norm_rows(m, h):
                s0 = 2 * h
                k = 4 * m + s0
                dve.wait_ge(S_["a_norm"], k)
                dve.wait_ge(S_["a_mv"], k)
                rows_in(dve, m, s0)
                nc.vector.bn_stats(stat[:, 0, :], rows_of(m, s0)).then_inc(S_["a_stat"], 1)
                rows_in(dve, m, s0 + 1)
                dve.wait_ge(S_["a_stat"], k + 1)
                nc.vector.bn_stats(stat[:, 1, :], rows_of(m, s0 + 1)).then_inc(S_["a_stat"], 1)
                nc.vector.bn_aggr(mvA[:, 0, :], stat[:, 0, :]).then_inc(S_["a_mv"], 1)
                dve.wait_ge(S_["a_stat"], k + 2)
                norm_a(m, s0)
                nc.vector.bn_aggr(mvA[:, 1, :], stat[:, 1, :]).then_inc(S_["a_mv"], 1)
                norm_a(m, s0 + 1)

            def norm_a(m, s):
                k = 4 * m + s
                dve.wait_ge(S_["a_rstd"], k + 1)
                nc.vector.tensor_scalar(rows_of(m, s), rows_of(m, s), mvA[:, s % 2, 0:1], rsA[:, s % 2, 1:2],
                                        ALU.subtract, ALU.mult).then_inc(S_["a_norm"], 1)

            def gated(m, e, j):
                k = 4 * m + e
                dve.wait_ge(S_["gate_sig"], k + 1)
                if e < 2:
                    if not (isinstance(m, int) and m == 0):
                        dve.wait_ge(ug_out[e % 2], 32 * m)
                    if not isinstance(m, int):
                        dve.wait_ge(S_["out_ok"], START + 4 * (m - TPB))
                else:
                    dve.wait_ge(ug_out[e % 2], 32 * m + 16)
                nc.vector.scalar_tensor_tensor(out=ugo[:, e % 2, :], in0=hT_of(m)[:, e, :], scalar=1.0,
                                               in1=two[:, e % 2, :], op0=ALU.mult, op1=ALU.mult,
                                               accum_out=usum[:, e, j:j + 1]).then_inc(S_["ug_done"], 1)

            def u_total(bt, m):
                dve.wait_ge(S_["ug_done"], 4 * m + 4)
                nc.vector.reduce_sum(umean[:, :], usum[:, :, :], mybir.AxisListType.X).then_inc(S_["um_done"], 1)

            def new_coef(bt):
                dve.wait_ge(S_["lr_in"], 16 * (1 + DC))
                dve.wait_ge(S_["lr_mm"], bt + 1)
                by_rank = bank_of(("lr", 0), 0, True)[:, 0:RANK].unsqueeze(1).broadcast_to([P, DC, RANK])
                nc.vector.tensor_tensor(lrp[:, :, :], by_rank, lrv[:, :, :], ALU.mult).then_inc(S_["lr_prod"], 1)
                dve.wait_ge(S_["lr_prod"], bt + 1)
                nc.vector.reduce_sum(dlr[:, :], lrp[:, :, :], mybir.AxisListType.X).then_inc(S_["lr_sum"], 1)
                dve.wait_ge(S_["lr_sum"], bt + 1)
                nc.vector.scalar_tensor_tensor(out=deff[:, :], in0=dlr[:, :],
                                               scalar=1.0 / (T * max(1.0, float(RANK))), in1=vec[:, 3, :],
                                               op0=ALU.mult, op1=ALU.add).then_inc(S_["d_eff"], 1)
                ga = modT[:, bt, GA, :] if isinstance(bt, int) else \
                    modT[:, bass.ds(bt, 1), GA, :].rearrange("p o c -> p (o c)")
                nc.vector.tensor_tensor(coef[:, 0, :], bc_[:, :], ga, ALU.mult).then_inc(S_["d_tmp"], 1)
                dve.wait_ge(S_["d_eff"], bt + 1)
                nc.vector.tensor_tensor(coef[:, 1, :], deff[:, :], ga, ALU.mult).then_inc(S_["coef_ok"], 1)

            def scan(r, e, j):
                k = 4 * r + e
                if e == 0:
                    dve.wait_ge(ug_in, 16 * r + 16)
                    bt = bt_of(r)
                    dve.wait_ge(S_["coef_ok"], bt + 1)
                    dve.wait_ge(S_["d_tmp"], bt + 1)
                if e < 2:
                    if not (isinstance(r, int) and r == 0):
                        dve.wait_ge(S_["hT2_mm"], 4 * r)
                        dve.wait_ge(y_out[2 + e], START + 16 * (r - 1))
                    dve.wait_ge(S_["ug_done"], scan_floor(r, e))
                else:
                    dve.wait_ge(S_["yT_ok"], k - 1)
                st = two[:, e % 2, :]
                if j == 0:
                    bt = bt_of(r)
                    nc.vector.tensor_tensor(st[:, 0:1], chan[:, e, 0:1], f0[:, e:e + 1],
                                            ALU.mult).then_inc(S_["p_first"], 1)
                    dve.wait_ge(S_["p_first"], 4 * bt + e + 1)
                    nc.vector.tensor_tensor_scan(st[:, 1:TOK], aa[:, e:e + 1].broadcast_to([P, TOK - 1]),
                                                 chan[:, e, 1:TOK], st[:, 0:1], ALU.mult, ALU.add
                                                 ).then_inc(S_["p_scan"], 1)
                else:
                    dve.wait_ge(S_["carry_ok"], 4 * (r - 1) + e + 1)
                    nc.vector.tensor_tensor_scan(st, aa[:, e:e + 1].broadcast_to([P, TOK]), chan[:, e, :],
                                                 carry[:, e:e + 1], ALU.mult, ALU.add).then_inc(S_["p_scan"], 1)
                dve.wait_ge(S_["p_scan"], k + 1)
                nc.vector.tensor_copy(carry[:, e:e + 1], st[:, TOK - 1:TOK]).then_inc(S_["carry_ok"], 1)
                nc.vector.tensor_scalar(chan[:, e, :], chan[:, e, :], coef[:, 1, e:e + 1], None,
                                        ALU.mult).then_inc(S_["p_mul"], 1)
                dve.wait_ge(S_["p_mul"], k + 1)
                nc.vector.scalar_tensor_tensor(out=chan[:, e, :], in0=st, scalar=coef[:, 0, e:e + 1],
                                               in1=chan[:, e, :], op0=ALU.mult, op1=ALU.add
                                               ).then_inc(S_["yT_ok"], 1)

            def scan_floor(r, e):
                if isinstance(r, int):
                    return 4 * min(r + TPB, NB * TPB) if r else 4 * TPB
                return 4 * (r + TPB)

            def add_x(r, s, after=None):
                k = 4 * r + s
                dve.wait_ge(S_["yT_mm"], k + 1)
                dve.wait_ge(xb_in[s % 2], 32 * r + 16 * (s // 2) + 16)
                if after is not None:
                    dve.wait_ge(S_["p_stat"], 4 * r + after + 1)
                nc.vector.tensor_tensor(xb[:, s % 2, :], bank_of(("yT", s), 0, True)[:, :], xb[:, s % 2, :],
                                        ALU.add).then_inc(S_["x_new"], 1)
                if after is not None:
                    aggr_p(r, after)
                dve.wait_ge(S_["x_new"], k + 1)
                if not (isinstance(r, int) and k < 2):
                    dve.wait_ge(S_["p_mv"], k - 1)
                    dve.wait_ge(S_["p_norm"], k - 1)
                nc.vector.bn_stats(stat[:, 2 + s % 2, :], xb[:, s % 2, :]).then_inc(S_["p_stat"], 1)

            def aggr_p(r, s):
                nc.vector.bn_aggr(mvP[:, s % 2, :], stat[:, 2 + s % 2, :]).then_inc(S_["p_mv"], 1)

            def norm_p(r, s, after=None):
                k = 4 * r + s
                dve.wait_ge(S_["p_rstd"], k + 1)
                if s < 2:
                    dve.wait_ge(S_["yT_ok"], 4 * r + 4)
                else:
                    dve.wait_ge(S_["hT2_mm"], k - 1)
                if after is not None:
                    dve.wait_ge(S_["p_stat"], 4 * r + after + 1)
                dst = two[:, s % 2, :].rearrange("p (g j w) -> p g w j", j=8, w=WPG)
                src = xb[:, s % 2, :].rearrange("p (g w j) -> p g w j", j=8, w=WPG)
                nc.vector.tensor_scalar(dst, src, mvP[:, s % 2, 0:1], rsP[:, s % 2, 1:2],
                                        ALU.subtract, ALU.mult).then_inc(S_["p_norm"], 1)
                if after is not None:
                    aggr_p(r, after)

            def split_x(r, c_):
                dve.wait_ge(S_["x1_ok"], 4 * r + c_ + 1)
                nc.vector.tensor_tensor(X2[:, c_, :], chan[:, c_, :], X1[:, c_, :].bitcast(F32),
                                        ALU.subtract).then_inc(S_["x2_ok"], 1)

            def chunk_h(n, i, between=None):
                q = NCH * n + i
                s_ = S[:, i % 2, :]
                dve.wait_ge(S_["sig_ok"], q + 1)
                nc.vector.scalar_tensor_tensor(out=s_, in0=gps[:, :], scalar=SHIFT_UP, in1=s_,
                                               op0=ALU.mult, op1=ALU.mult).then_inc(S_["gs_ok"], 1)
                if between is not None:
                    between()
                dve.wait_ge(S_["u_mm"], q + 1)
                dve.wait_ge(S_["gs_ok"], START + q + 1)
                nc.vector.scalar_tensor_tensor(out=s_, in0=ups[:, :], scalar=SHIFT_UP, in1=s_,
                                               op0=ALU.mult, op1=ALU.mult).then_inc(S_["h_ok"], 1)

            def final(n, bt, subs):
                for s in subs:
                    if s == 0:
                        dve.wait_ge(S_["gb_in"], 16 * bt + 16)
                        dve.wait_ge(S_["out_ok"], START + 4 * n)
                    if s < 2:
                        done = min(n + 1 + TPB, NB * TPB) if isinstance(n, int) else n + 1 + TPB
                        dve.wait_ge(ug_out[s], 32 * done)
                    dve.wait_ge(S_["rms_ok"], 4 * n + s + 1)
                    nc.vector.scalar_tensor_tensor(out=yo[s], in0=yps[s][:, :], scalar=rms[:, s, 1:2],
                                                   in1=gbB[:, :], op0=ALU.mult, op1=ALU.mult
                                                   ).then_inc(S_["y_used"], 1)

            cur = {}

            def bt_of(t):
                return t // TPB if isinstance(t, int) else cur["bt_" + str(cur["which"])]

            dve.wait_ge(S_["csig_ok"], 1)
            nc.vector.tensor_tensor(csig, csig, crow, ALU.mult).then_inc(S_["silu_ok"], 1)
            norm_rows(0, 0)
            norm_rows(0, 1)

            dve.wait_ge(S_["vec_tanh"], 1)
            nc.vector.tensor_scalar(f0[:, :], aa[:, :], 1e-6, None, ALU.max).then_inc(S_["vec_fix"], 1)
            nc.vector.tensor_tensor(bc_[:, :], vec[:, 1, :], vec[:, 2, :], ALU.mult).then_inc(S_["vec_fix"], 1)
            dve.wait_ge(S_["vec_fix"], 2)
            nc.vector.reciprocal(f0[:, :], f0[:, :]).then_inc(S_["vec_fix"], 1)
            dve.wait_ge(S_["vec_fix"], 3)
            nc.vector.tensor_tensor(f0[:, :], f0[:, :], aa[:, :], ALU.mult).then_inc(S_["vec_fix"], 1)
            dve.wait_ge(S_["vec_fix"], 4)

            def mod_fix(k, row):
                g_ = mrow[:, D * row:D * (row + 1)]
                dve.wait_ge(S_["mod_row"], MODS.index(row) + 1)
                nc.vector.tensor_scalar(mtmp[:, :], g_, 0.0, 2.0, ALU.is_ge, ALU.mult).then_inc(S_["mod_fix"], 1)
                dve.wait_ge(S_["mod_fix"], FIXES * k + 1)
                nc.vector.tensor_scalar(mtmp[:, :], mtmp[:, :], 1.0, None, ALU.subtract).then_inc(S_["mod_fix"], 1)
                nc.vector.scalar_tensor_tensor(out=g_, in0=g_, scalar=-1.0, in1=g_,
                                               op0=ALU.mult, op1=ALU.max).then_inc(S_["mod_fix"], 1)
                dve.wait_ge(S_["mod_fix"], FIXES * k + 3)
                nc.vector.scalar_tensor_tensor(out=g_, in0=g_, scalar=0.25, in1=mtmp[:, :],
                                               op0=ALU.max, op1=ALU.mult).then_inc(S_["mod_fix"], 1)
                dve.wait_ge(S_["mod_fix"], FIXES * (k + 1))

            def dq_unpack(gi):
                kind, c0, n_ = GROUPS[gi]
                if gi == 0:
                    dve.wait_ge(S_["gpk_in"], 16 * 8)
                else:
                    if gi == DC:
                        dve.wait_ge(S_["dpk_in"], 16)
                    dve.wait_ge(S_["dq_mm"], GROUP_END[gi - 1])
                if kind == "gu":
                    words = gpk[:, :, WPG * c0:WPG * (c0 + 1)]
                    out_ = nib[:, :].rearrange("p (o j w) -> p o j w", j=8, w=WPG)
                    size = 2 * HID
                else:
                    words = dpk[:, :, WPG * c0:WPG * (c0 + n_)].rearrange("p h (c w) -> p h c w", w=WPG)
                    size = DC * n_ * P
                    out_ = nib[:, 0:size].rearrange("p (h c j w) -> p h c j w", c=n_, j=8, w=WPG)
                for j in range(8):
                    ins = nc.vector.tensor_scalar(out_[:, :, j, :] if kind == "gu" else out_[:, :, :, j, :], words,
                                                  28 - 4 * j, 3, ALU.logical_shift_left, ALU.arith_shift_right)
                ins.then_inc(S_["dq_top"], 1)
                dve.wait_ge(S_["dq_top"], gi + 1)
                nc.vector.tensor_scalar(nib[:, 0:size], nib[:, 0:size], -0x72000000, None,
                                        ALU.bitwise_and).then_inc(S_["dq_nib"], 1)

            def dq(uu):
                gi, b0, nb_, kind, ch, col = UNITS[uu]
                if uu >= 2:
                    dve.wait_ge(S_["dq_w2"], uu - 1)
                part = gi
                at = col if kind == "gu" else D * (ch - GROUPS[gi][1])
                dve.wait_ge(scl_in[part % 2], 16 * (part // 2) + 16)
                dve.wait_ge(S_["dq_mm"], uu + 1)
                scale, dst = scl[:, part % 2, at:at + P * nb_], raw[:, uu % 2, 0:P * nb_]
                val = dq_banks[uu % NDQ][:, :].bitcast(F16)[:, 0:P * nb_]
                if kind == "gu":
                    scale = scale.rearrange("p (c w j) -> p c j w", w=WPG, j=8)
                    val = val.rearrange("p (c j w) -> p c j w", w=WPG, j=8)
                    dst = dst.rearrange("p (c j w) -> p c j w", w=WPG, j=8)
                nc.vector.tensor_tensor(dst, val, scale, ALU.mult).then_inc(S_["dq_raw"], 1)

            cur["which"] = "p"
            for item in PROLOGUE:
                kind, q = item[0], item[1]
                if kind == "norm":
                    norm_rows(q, item[2])
                elif kind == "gate":
                    gated(q, item[2], q)
                elif kind == "unpack":
                    dq_unpack(q)
                elif kind == "dq":
                    dq(q)
                elif kind == "fix":
                    mod_fix((GA, GB).index(MODS[q]), MODS[q])
                elif kind == "sum":
                    u_total(0, TPB - 1)
                elif kind == "deff":
                    dve.wait_ge(S_["modt_ok"], len(MOD_T))
                    new_coef(0)
                elif kind == "scan":
                    scan(0, q, 0)
                elif kind == "yT":
                    if q == 2:
                        norm_p(0, 0, after=1)
                    if q == 3:
                        norm_p(0, 1, after=2)
                    add_x(0, q, after={1: 0}.get(q))
                elif item == ("hT2", 1):
                    norm_p(0, 2, after=3)
                    norm_p(0, 3)
            for c_ in range(DC):
                split_x(0, c_)

            def step(n, j, bt, with_a, with_p):
                m, r = n + TPB, n + 1
                cur["bt_p"] = bt + 1 if j == TPB - 1 else bt
                for i in range(NCH):
                    if i == 0 and j:
                        chunk_h(n, i, between=lambda: final(n - 1, bt, (NSUB - 1,)))
                    else:
                        chunk_h(n, i)
                    if with_a:
                        if i in (0, 1):
                            norm_rows(m, i)
                        if i in (3, 4):
                            for e in (2 * i - 6, 2 * i - 5):
                                gated(m, e, j)
                        if i == 4 and j == TPB - 1:
                            u_total(bt + 1, m)
                        if i == 5 and j == TPB - 1:
                            new_coef(bt + 1)
                    if with_p:
                        turns = {5: (0,), 6: (1, 2, 3)} if j == TPB - 1 else {5: (0, 1), 6: (2, 3)}
                        for e in turns.get(i, ()):
                            scan(r, e, (j + 1) % TPB)
                        if i == 7:
                            add_x(r, 0)
                            add_x(r, 1, after=0)
                            norm_p(r, 0, after=1)
                        if i == 8:
                            add_x(r, 2)
                            norm_p(r, 1, after=2)
                        if i == 9:
                            add_x(r, 3)
                            norm_p(r, 2, after=3)
                            norm_p(r, 3)
                if with_p:
                    for c_ in range(DC):
                        split_x(r, c_)
                final(n, bt, range(NSUB if j == TPB - 1 else NSUB - 1))

            with dve.Fori(0, NB - 1) as bt:
                for j in range(TPB):
                    step(TPB * bt + j, j, bt, True, True)
            for j in range(TPB):
                step(TPB * (NB - 1) + j, j, NB - 1, False, j < TPB - 1)

        @block.tensor
        def _(pe):
            for first in STARTED["pe"]:
                pe.sem_inc(first, START)

            def attn_T(bk, m, s):
                dst = bk.take(pe, ("xT", s), m=m)
                pe.wait_ge(S_["a_norm"], 4 * m + s + 1)
                for c_ in range(DC):
                    ins = nc.tensor.transpose(dst[:, P * c_:P * (c_ + 1)], rows_of(m, s)[:, P * c_:P * (c_ + 1)], ident[:, :])
                ins.then_inc(S_["xT_mm"], 1)

            def gate(bk, m, e):
                dst = bk.take(pe, ("gate", e), m=m)
                pe.wait_ge(S_["hT_ok"], 4 * m + 4)
                for k in range(DC):
                    ins = nc.tensor.matmul(dst[:, :], WG[:, k, P * e:P * (e + 1)], hT_of(m)[:, k, :],
                                           start=(k == 0), stop=(k == DC - 1))
                ins.then_inc(S_["gate_mm"], 1)

            def low_rank(bk, bt):
                dst = bk.take(pe, ("lr", 0), bt=bt)
                pe.wait_ge(S_["um_done"], bt + 1)
                for k in range(DC):
                    ins = nc.tensor.matmul(dst[:, 0:RANK], umean[:, k:k + 1].broadcast_to([P, P]), lru[:, k, :],
                                           start=(k == 0), stop=(k == DC - 1))
                ins.then_inc(S_["lr_mm"], 1)

            def y_T(bk, r, s):
                dst = bk.take(pe, ("yT", s), r=r)
                pe.wait_ge(S_["yT_ok"], 4 * r + 4)
                for e in range(DC):
                    ins = nc.tensor.transpose(dst[:, P * e:P * (e + 1)], chan[:, e, P * s:P * (s + 1)], ident[:, :])
                ins.then_inc(S_["yT_mm"], 1)

            def h_T(bk, r, s):
                dst = bk.take(pe, ("hT2", s), r=r)
                pe.wait_ge(S_["p_norm"], 4 * r + s + 1)
                for c_ in range(DC):
                    ins = nc.tensor.transpose(dst[:, P * c_:P * (c_ + 1)], two[:, s % 2, P * c_:P * (c_ + 1)], ident[:, :])
                ins.then_inc(S_["hT2_mm"], 1)

            def piece(bk, p, n, bt):
                kind, s = p
                if kind == "xT":
                    attn_T(bk, n + TPB, s)
                elif kind == "gate":
                    gate(bk, n + TPB, s)
                elif kind == "lr":
                    low_rank(bk, bt + 1)
                elif kind == "yT":
                    y_T(bk, n + 1, s)
                else:
                    h_T(bk, n + 1, s)

            def project(dst, col, n, first, done):
                for k in range(DC):
                    if first:
                        pe.wait_ge(S_["x1_ok"], 4 * n + k + 1)
                    for w in (W1, W2):
                        nc.tensor.matmul(dst[:, :], w[:, k, col:col + P], X1[:, k, :],
                                         start=(k == 0 and w is W1), stop=False)
                for k in range(DC):
                    if first:
                        pe.wait_ge(S_["x2_ok"], 4 * n + k + 1)
                    ins = nc.tensor.matmul(dst[:, :], W1[:, k, col:col + P], X2[:, k, :],
                                           start=False, stop=(k == DC - 1))
                ins.then_inc(S_[done], 1)

            def down(n, i):
                q = NCH * n + i
                pe.wait_ge(S_["h1_ok"], q + 1)
                if i == 0:
                    pe.wait_ge(S_["y_used"], START + 4 * n)
                for s in range(NSUB):
                    for v in (V1, V2):
                        nc.tensor.matmul(yps[s][:, :], H1[:, i % 2, P * s:P * (s + 1)], v[:, i, :],
                                         start=(i == 0 and v is V1), stop=False)
                pe.wait_ge(S_["h2_ok"], START + q + 1)
                for s in range(NSUB):
                    ins = nc.tensor.matmul(yps[s][:, :], H2[:, i % 2, P * s:P * (s + 1)], V1[:, i, :],
                                           start=False, stop=(i == NCH - 1))
                    if i == NCH - 1:
                        ins.then_inc(S_["y_mm"], 1)
                if i < NCH - 1:
                    ins.then_inc(S_["d_mm"], 1)

            pe.wait_ge(S_["ident_ok"], 2)
            pe.wait_ge(S_["silu_ok"], 1)
            for k in range(DC):
                ins = nc.tensor.transpose(bank[0][:, NB * k:NB * (k + 1)], csig[:, P * k:P * (k + 1)],
                                          ident[0:NB, 0:NB])
            ins.then_inc(S_["cT_mm"], 1)

            def mod(t):
                if t >= 1:
                    pe.wait_ge(S_["mod_row"], t)
                prior = [x for x in MOD_T if x < t]
                if prior:
                    pe.wait_ge(S_["modt_ok"], MOD_T.index(prior[-1]) + 1)
                pe.wait_ge(wm_in[t % 2], 16 * (t // 2) + 16)
                for k in range(DC):
                    ins = nc.tensor.matmul(modps[0:NB, :], cT[:, k, :], wm[:, t % 2, k, :],
                                           start=(k == 0), stop=(k == DC - 1))
                ins.then_inc(S_["mod_mm"], 1)

            def mod_T(t):
                i = MODS[t]
                pe.wait_ge(S_["mod_row"], t + 1)
                if i == GA:
                    pe.wait_ge(S_["mod_fix"], FIXES)
                for c_ in range(DC):
                    ins = nc.tensor.transpose(modps[:, NB * c_:NB * (c_ + 1)],
                                              mrow[:, D * i + P * c_:D * i + P * (c_ + 1)], ident[0:NB, 0:NB])
                ins.then_inc(S_["modt_mm"], 1)

            pe.wait_ge(S_["cT_ok"], 1)
            mod(0)
            mod_T(0)
            mod(1)
            mod_T(1)
            pe.wait_ge(S_["gw_in"], 16)
            for k in range(DC):
                if k >= 2:
                    pe.wait_ge(S_["gw_ok"], k - 1)
                for e in range(DC):
                    ins = nc.tensor.transpose(bank[k % 2][:, P * e:P * (e + 1)], gwr[:, e, P * k:P * (k + 1)],
                                              ident[:, :])
                ins.then_inc(S_["gw_mm"], 1)
            pe.wait_ge(S_["gw_ok"], DC)

            def dq(uu):
                gi, b0, nb_, kind, ch, col = UNITS[uu]
                if uu >= NDQ:
                    pe.wait_ge(S_["dq_raw"], uu - NDQ + 1)
                pe.wait_ge(S_["dq_nib"], gi + 1)
                dst = dq_banks[uu % NDQ][:, :].bitcast(F16)
                for i, blk in enumerate(dq_blocks(uu)):
                    ins = nc.tensor.transpose(dst[:, P * i:P * (i + 1)], blk, ident16[:, :])
                ins.then_inc(S_["dq_mm"], 1)

            bk, bk_xT = Banks(), Banks(xT_banks)
            for item in PROLOGUE:
                kind, q = item[0], item[1]
                if kind == "xT":
                    attn_T(bk_xT, q, item[2])
                elif kind == "gate":
                    gate(bk, q, item[2])
                elif kind == "dq":
                    dq(q)
                elif kind == "mod":
                    mod(q)
                elif kind == "modT":
                    mod_T(q)
                elif kind == "deff":
                    pe.wait_ge(S_["lr_in"], 16 * (1 + DC))
                    low_rank(bk, 0)
                elif kind == "yT":
                    y_T(bk, 0, q)
                elif kind == "hT2":
                    h_T(bk, 0, q)
            pe.wait_ge(S_["dq_w2"], NU)

            SLOT = {1: [("xT", 0), ("xT", 1)], 2: [("xT", 2), ("xT", 3)], 3: [("gate", 0), ("gate", 1)],
                    4: [("gate", 2), ("gate", 3)], 5: [("lr", 0)],
                    7: [("yT", 0), ("yT", 1)], 8: [("yT", 2), ("hT2", 0)], 9: [("yT", 3), ("hT2", 1)],
                    10: [("hT2", 2), ("hT2", 3)]}

            def wanted(p, j, with_a, with_p):
                kind = p[0]
                if kind in ("xT", "gate"):
                    return with_a
                if kind == "lr":
                    return with_a and j == TPB - 1
                return with_p

            def step(bk, n, j, bt, with_a, with_p):
                for i in range(NCH):
                    q = NCH * n + i
                    pe.wait_ge(S_["gs_ok"], START + q)
                    project(gps, P * i, n, i == 0, "g_mm")
                    pe.wait_ge(S_["h_ok"], START + q)
                    project(ups, HID + P * i, n, i == 0, "u_mm")
                    ps = [p for p in SLOT.get(i, []) if wanted(p, j, with_a, with_p)]
                    for p in ps[:1]:
                        piece(bk, p, n, bt)
                    if i:
                        down(n, i - 1)
                    for p in ps[1:]:
                        piece(bk, p, n, bt)
                down(n, NCH - 1)

            with pe.Fori(0, NB - 1) as bt:
                bk.hist = [(("hT2", 2), None, TPB * bt, None), (("hT2", 3), None, TPB * bt, None)]
                for j in range(TPB):
                    step(bk, TPB * bt + j, j, bt, True, True)
            bk = Banks()
            bk.hist = [(("hT2", 2), None, TPB * (NB - 1), None), (("hT2", 3), None, TPB * (NB - 1), None)]
            for j in range(TPB):
                step(bk, TPB * (NB - 1) + j, j, NB - 1, False, j < TPB - 1)


_INS = ['L0_attn_u', 'L0_attn_a', 'L0_attn_b', 'L0_attn_c', 'L0_attn_d', 'L0_attn_gate_w', 'L0_attn_gate_b',
        'L0_attn_d_lr_u', 'L0_attn_d_lr_v', 'L0_ffn_gate_up_packed', 'L0_ffn_gate_up_scales',
        'L0_ffn_down_packed', 'L0_ffn_down_scales', 'L0_c', 'L0_wmod']


def kernel(**inputs):
    import numpy as _np
    import concourse.bacc as _bacc
    from concourse import mybir as _mybir
    from concourse.bass_utils import run_bass_kernel_spmd as _run

    nc = _bacc.Bacc("TRN2", target_bir_lowering=False, num_devices=1)
    arrays, args = {}, []
    for name in _INS:
        a = _np.ascontiguousarray(inputs[name])
        arrays[f"in_{name}_dram"] = a
        args.append(nc.dram_tensor(f"in_{name}_dram", a.shape, _mybir.dt.from_np(a.dtype), kind="ExternalInput").ap())
    shape = tuple(inputs['L0_attn_u'].shape)
    args.append(nc.dram_tensor("out_0_dram", shape, _mybir.dt.from_np(_np.dtype('float32')), kind="ExternalOutput").ap())
    adaln_block_kernel(nc, *args)
    r = _run(nc, [arrays], core_ids=[0])
    return r.results[0]["out_0_dram"]
```

```python
import numpy as np
import concourse.bass as bass
from concourse import mybir
from contextlib import ExitStack

F32 = mybir.dt.float32
F32R = mybir.dt.float32r
F16 = mybir.dt.float16
I32 = mybir.dt.int32
ALU = mybir.AluOpType
ACT = mybir.ActivationFunctionType

P = 128


def adaln_block_kernel(nc, u, a, b, c, d, gate_w, gate_b, d_lr_u, d_lr_v,
                       gu_packed, gu_scales, dn_packed, dn_scales, cond, wmod, out):
    NB, T, D = u.shape
    HID = gu_packed.shape[0] // 2
    RANK = d_lr_u.shape[1]
    NMOD = wmod.shape[1] // D
    TOK = 512
    NSUB = TOK // P
    TPB = T // TOK
    DC = D // P
    NCH = HID // P
    WPG = P // 8
    SHIFT_UP = 2.0 ** 14
    LN_EPS = 1e-5
    RMS_EPS = 1e-6
    SA, CA, GA, SB, CB, GB = range(6)

    xv = u.rearrange("b (j s p) d -> (b j) s p d", p=P, s=NSUB)
    ov = out.rearrange("b (j s p) d -> (b j) s p d", p=P, s=NSUB)

    ug_dram = nc.dram_tensor("ug_scratch", [NB * TPB, P, DC, TOK], F32).ap()
    xn_dram = nc.dram_tensor("xnew_scratch", [NB * TPB, NSUB, P, D], F32).ap()
    gb_dram = nc.dram_tensor("gb_scratch", [NB, D], F32).ap()

    with ExitStack() as ctx:
        def sb(name, shape, dt, scope=ctx):
            return scope.enter_context(nc.sbuf_tensor(name, shape, dt))

        def pb(name):
            return ctx.enter_context(nc.psum_tensor(name, [P, 512], F32))

        def sem(name):
            return ctx.enter_context(nc.semaphore(name))

        W1 = sb("gu_w1", [P, DC, 2 * HID], F32R)
        W2 = sb("gu_w2", [P, DC, 2 * HID], F32R)
        with ExitStack() as early:
            WG = sb("gate_wT", [P, DC, D], F32, early)
        WG2 = sb("gate_w2", [P, DC, D], F32R)
        with ExitStack() as shared:
            chan = sb("chan", [P, DC, TOK], F32, shared)
            rows = sb("rows", [P, DC, TOK], F32, shared)
        h_lo = sb("h_lo", [P, DC, TOK], F32R)
        h_hi = sb("h_hi", [P, DC, TOK], F32R)
        xb = sb("xb", [P, 2, D], F32)
        two = sb("two", [P, 2, D], F32)
        ugo = sb("ugo", [P, 2, TOK], F32)
        ident = sb("ident", [P, P], F32)
        vec = sb("vec", [P, 5, DC], F32)
        modT = sb("modT", [P, NB, 5, DC], F32)
        modA = sb("modA", [P, 2, DC], F32)
        modP = sb("modP", [P, 2, DC], F32)
        coef = sb("coef", [P, 2, DC], F32)
        usum = sb("usum", [P, DC, TPB], F32)
        umean = sb("umean", [P, DC], F32)
        lru = sb("lru", [P, DC, RANK], F32)
        lrv = sb("lrv", [P, DC, RANK], F32)
        lrp = sb("lrp", [P, DC, RANK], F32)
        carry = sb("carry", [P, DC], F32)
        stat = sb("stat", [P, 4, 6], F32)
        mvA = sb("mvA", [P, 2, 2], F32)
        mvP = sb("mvP", [P, 2, 2], F32)
        rsA = sb("rsA", [P, 2, 2], F32)
        rsP = sb("rsP", [P, 2, 2], F32)
        ssq = sb("ssq", [P, NSUB], F32)
        rms = sb("rms", [P, NSUB, 2], F32)
        consts = sb("consts", [P, 3], F32)
        k_pow = consts[:, 0:1]
        k_eps = consts[:, 1:3]
        vecs = sb("vecs", [P, 5, DC], F32)
        aa = vecs[:, 0, :]
        f0 = vecs[:, 1, :]
        bc_ = vecs[:, 2, :]
        dlr = vecs[:, 3, :]
        deff = vecs[:, 4, :]
        cT = sb("cT", [P, DC, NB], F32)
        crow, csig = xb[0:NB, 0, :], xb[0:NB, 1, :]

        with ExitStack() as early:
            wm = sb("wm", [P, 2, DC, D], F32, early)
            mrow = sb("mrow", [NB, NMOD * D], F32, early)
            mtmp = sb("mtmp", [NB, D], F32, early)
            at_end = (NCH * 2 * D - 2 * DC * D - NMOD * D - D - DC * TOK)
            sb("unused", [P, at_end], F32, early)
            chan_b = sb("chan_b", [P, DC, TOK], F32, early)
            gwr = chan_b
        V1 = sb("dn_w1", [P, NCH, D], F32R)
        V2 = sb("dn_w2", [P, NCH, D], F32R)
        with ExitStack() as early:
            gpk = sb("gu_words", [P, 2 * NCH, D // 8], I32, early)
            dpk = sb("dn_words", [P, DC, HID // 8], I32, early)
            scl = sb("scales", [P, 2, 2 * HID], F16, early)
            raw = sb("raw", [P, 2, 512], F32, early)
            nib = sb("nib", [P, 2 * HID], I32, early)
            ident16 = sb("ident16", [P, P], F16, early)
        X1 = sb("ffn_x1", [P, DC, TOK], F32R)
        X2 = sb("ffn_x2", [P, DC, TOK], F32R)
        S = sb("silu_up", [P, 2, TOK], F32)
        H1 = sb("h1", [P, 2, TOK], F32R)
        H2 = sb("h2", [P, TOK], F32R)
        WG1 = sb("gate_hi", [P, DC, D], F32R)
        gbB = sb("gb_rows", [P, D], F32)
        fin = [xb[:, 0, :], xb[:, 1, :], two[:, 0, :], two[:, 1, :]]

        bank = [pb("bank0"), pb("bank1")]
        gps = pb("gate_ps")
        ups = pb("up_ps")
        yps = [pb(f"y_ps{s}") for s in range(NSUB)]
        dq_banks = [ups] + yps[0:2]
        xT_banks = yps[2:4]
        NDQ = len(dq_banks)
        modps = gps

        S_ = {n: sem(n) for n in """
            cond_in vec_in lr_in gw_in gpk_in dpk_in ident_ok const_ok
            csig_ok silu_ok cT_mm cT_ok mod_mm mod_row modt_mm modt_ok mod_fix gb_saved
            gw_mm gw_ok vec_tanh vec_fix
            dq_mm dq_top dq_nib dq_raw dq_w1 dq_w2
            a_stat a_mv a_eps a_rstd a_norm xT_mm hT_ok modA_ok gate_mm gate_sig ug_done
            h1a_ok h2a_ok hsum_ok g_hi g_lo um_done lr_mm lr_prod lr_sum d_eff d_tmp coef_ok
            p_first p_scan carry_ok p_mul yT_ok yT_mm x_new p_stat p_mv p_eps p_rstd p_norm hT2_mm modP_ok x_next
            x1_ok x2_ok g_mm u_mm sig_ok gs_ok h_ok h1_ok h2_ok d_mm
            y_mm sq_ok rms_a rms_ok y_used out_ok gb_in
        """.split()}
        wm_in = [sem(f"wm_in{i}") for i in range(2)]
        scl_in = [sem(f"scl_in{i}") for i in range(2)]
        xa_in = [sem(f"xa_in{i}") for i in range(NSUB)]
        xb_in = [sem(f"xb_in{i}") for i in range(2)]
        fin_in = [sem(f"fin_in{i}") for i in range(NSUB)]
        ug_out = [sem(f"ug_out{i}") for i in range(2)]
        ug_in = sem("ug_in")
        xn_out = [sem(f"xn_out{i}") for i in range(2)]
        y_out = [sem(f"y_out{i}") for i in range(NSUB)]

        START = 1
        STARTED = {"dve": [S_[k] for k in ("gs_ok", "h_ok", "y_used")],
                   "pool": [S_[k] for k in ("out_ok", "h2_ok")],
                   "pe": [S_[k] for k in ("y_mm", "d_mm")], "sp": y_out, "act": [S_["sq_ok"]]}

        def early_tile(m):
            return isinstance(m, int) and m < TPB

        def hT_of(m):
            return chan_b if early_tile(m) and m % 2 else chan

        def wide(j, with_a):
            return not with_a or j == TPB - 1

        def yo(s, j, with_a):
            return rows[:, s, :] if s >= 2 and wide(j, with_a) else ugo[:, s % 2, :]

        def late(j, with_a):
            return () if j == TPB - 1 else (2, 3) if with_a else (3,)

        GROUPS = [("gu", g, 1) for g in range(DC)] + [("dn", c_, min(4, NCH - c_)) for c_ in range(0, NCH, 4)]
        FIXES = 4
        UNITS = []
        for gi, (kind, c0, nc_) in enumerate(GROUPS):
            if kind == "gu":
                UNITS += [(gi, o, min(4, 2 * NCH - o), kind, c0, P * o) for o in range(0, 2 * NCH, 4)]
            else:
                UNITS += [(gi, c_, DC, kind, c0 + c_, 0) for c_ in range(nc_)]
        NU = len(UNITS)
        FIRST_UNDER_END = NU - NCH + (NCH * D - DC * TOK) // D
        GROUP_END = [sum(1 for x in UNITS if x[0] <= gi) for gi in range(len(GROUPS))]

        def dq_blocks(uu):
            gi, b0, nb_, kind, ch, col = UNITS[uu]
            n_ = GROUPS[gi][2]
            v = nib[:, :].bitcast(F16)
            for i in range(nb_):
                blk = b0 + i if kind == "gu" else i * n_ + b0
                yield v[:, 2 * P * blk + 1:2 * P * (blk + 1):2]

        def dq_dst(uu, which):
            gi, b0, nb_, kind, ch, col = UNITS[uu]
            w = (W1, W2) if kind == "gu" else (V1, V2)
            return w[which][:, ch, col:col + P * nb_]

        MODS = [CA, SA, GA, GB, CB, SB]
        PROLOGUE = []
        todo, unpacked = list(range(NU)), set()

        def some(n_, may_unpack=True):
            steps = []
            while todo and len(steps) < n_:
                first = todo[0] == 0 or UNITS[todo[0]][0] != UNITS[todo[0] - 1][0]
                if first and UNITS[todo[0]][0] not in unpacked:
                    if not may_unpack:
                        break
                    unpacked.add(UNITS[todo[0]][0])
                    steps.append(("unpack", UNITS[todo[0]][0]))
                elif todo[0] >= FIRST_UNDER_END and ("gate", TPB - 1, DC - 1) not in PROLOGUE:
                    break
                else:
                    steps.append(("dq", todo.pop(0)))
            return steps

        MOD_STEPS = {0: [("mod", 2)], 1: [("fix", 2), ("modT", 2)], 2: [("mod", 3)], 3: [("fix", 3), ("mod", 4)],
                     4: [("modT", 4), ("mod", 5)], 5: [("modT", 5)]}
        PROLOGUE += [("xT", 0, s) for s in range(NSUB)] + some(2)
        for m in range(TPB):
            for e in range(DC):
                if m + 1 < TPB and m:
                    PROLOGUE += [("xT", m + 1, e)]
                PROLOGUE += some(1)
                if m == 0 and e == 0:
                    PROLOGUE += [("norm", 1, 0)]
                if m == 0 and e == 2:
                    PROLOGUE += [("norm", 1, 1)]
                if e == 0 and 1 < m + 1 < TPB:
                    PROLOGUE += [("norm", m + 1, 1)]
                if e == DC - 1 and m + 2 < TPB:
                    PROLOGUE += [("norm", m + 2, 0)]
                PROLOGUE += [("gate", m, e)] + MOD_STEPS.get(DC * m + e, [])
                if m == 0:
                    PROLOGUE += [("xT", 1, e)]
                PROLOGUE += some(1 + (m > 0), may_unpack=False)
        PROLOGUE += [("sum", 0)] + some(2) + [("deff", 0)]
        for e in range(DC):
            PROLOGUE += [("scan", e)] + some(1, may_unpack=False)
        PROLOGUE += [("yT", 0), ("yT", 1)] + some(1) + [("yT", 2)] + some(1) + [("hT2", 0), ("yT", 3)]
        PROLOGUE += some(2) + [("hT2", 1)] + some(1) + [("hT2", 2)] + some(1) + [("hT2", 3)] + some(2 * NU)

        MOD_T = [0, 1] + [x[1] for x in PROLOGUE if x[0] == "modT"]

        A_ORDER = [("xT", 0), ("xT", 1), ("xT", 2), ("xT", 3), ("gate", 0), ("gate", 1), ("gate", 2), ("gate", 3)]
        P_ORDER = [("yT", 0), ("yT", 1), ("yT", 2), ("hT2", 0), ("yT", 3), ("hT2", 1), ("hT2", 2), ("hT2", 3)]

        def freed(eng, piece, m, r, bt):
            kind, s = piece
            if kind == "xT":
                eng.wait_ge(S_["hT_ok"], 4 * m + s + 1)
            elif kind == "gate":
                eng.wait_ge(S_["gate_sig"], 4 * m + s + 1)
            elif kind == "lr":
                eng.wait_ge(S_["lr_prod"], bt + 1)
            elif kind == "yT":
                eng.wait_ge(S_["x_new"], 4 * r + s + 1)
            else:
                eng.wait_ge(S_["x_next"], 4 * r + s + 1)

        class Banks:
            def __init__(self, banks=bank):
                self.hist, self.banks = [], banks

            def take(self, eng, piece, m=None, r=None, bt=None):
                if len(self.hist) >= 2:
                    freed(eng, *self.hist[-2])
                if piece[0] == "lr":
                    self.hist[-2] = (piece, m, r, bt)
                    return self.banks[0]
                self.hist.append((piece, m, r, bt))
                return self.banks[(len(self.hist) - 1) % 2]

        def bank_of(piece):
            order = {"xT": A_ORDER, "gate": A_ORDER, "lr": [piece]}.get(piece[0], P_ORDER)
            return bank[order.index(piece) % 2]

        block = ctx.enter_context(nc.Block())

        @block.sync
        def _(sp):
            for first in STARTED["sp"]:
                sp.sem_inc(first, START)
            wmv = wmod.rearrange("(k p) (i d) -> i p k d", p=P, d=D)

            def load_mod(t):
                if t >= 2:
                    sp.wait_ge(S_["mod_mm"], t - 1)
                sp.dma_start(wm[:, t % 2, :, :], wmv[MODS[t]]).then_inc(wm_in[t % 2], 16)

            def load_scales(gi):
                kind, c0, n_ = GROUPS[gi]
                if gi >= 2:
                    sp.wait_ge(S_["dq_raw"], GROUP_END[gi - 2])
                if kind == "gu":
                    src, size = gu_scales[c0:c0 + 1, :], 2 * HID
                else:
                    src, size = dn_scales[c0:c0 + n_, :].rearrange("g o -> (g o)").unsqueeze(0), n_ * D
                sp.dma_start(scl[:, gi % 2, 0:size], src.broadcast_to([P, size])).then_inc(scl_in[gi % 2], 16)

            def load_x_attn(m, s):
                if early_tile(m):
                    if m:
                        sp.wait_ge(S_["xT_mm"], 4 * m + s - 3)
                elif s == 0:
                    sp.wait_ge(S_["gate_mm"], 4 * m)
                sp.dma_start(rows[:, s, :], xv[m, s, :, :]).then_inc(xa_in[s], 16)

            sp.dma_start(crow, cond).then_inc(S_["cond_in"], 16)
            load_x_attn(0, 0)
            load_x_attn(0, 1)
            load_mod(0)
            load_x_attn(0, 2)
            load_x_attn(0, 3)
            load_mod(1)
            sp.dma_start(gwr[:, :, :], gate_w.rearrange("(c p) d -> p c d", p=P)).then_inc(S_["gw_in"], 16)
            gsrc = gu_packed.rearrange("(c w j) k -> j w c k", w=WPG, j=8)
            for j in range(8):
                sp.dma_start(gpk[WPG * j:WPG * (j + 1), :, :], gsrc[j]).then_inc(S_["gpk_in"], 16)
            load_scales(0)
            with nc.allow_non_contiguous_dma(reason="small vectors by channel"):
                for i, v in enumerate((a, b, c, d, gate_b)):
                    sp.dma_start(vec[:, i, :], v.rearrange("(c p) -> p c", p=P)).then_inc(S_["vec_in"], 16)
                for c_ in range(DC):
                    sp.dma_start(lrv[:, c_, :], d_lr_v[:, P * c_:P * (c_ + 1)].rearrange("r p -> p r")
                                 ).then_inc(S_["lr_in"], 16)
            load_scales(1)
            load_mod(2)
            sp.dma_start(lru[:, :, :], d_lr_u.rearrange("(c p) r -> p c r", p=P)).then_inc(S_["lr_in"], 16)
            sp.dma_start(dpk[:, :, :], dn_packed.rearrange("(c p) k -> p c k", p=P)).then_inc(S_["dpk_in"], 16)

            def store_ug(m, e):
                sp.wait_ge(S_["ug_done"], 4 * m + e + 1)
                sp.dma_start(ug_dram[m, :, e, :], ugo[:, e % 2, :]).then_inc(ug_out[e % 2], 16)

            def load_ug(r, m):
                if m is not None:
                    sp.wait_ge(S_["ug_done"], 4 * m + 4)
                else:
                    sp.wait_ge(S_["x2_ok"], 4 * r)
                for k in range(2):
                    sp.wait_ge(ug_out[k], 32 * r + 32)
                sp.dma_start(chan[:, :, :], ug_dram[r, :, :, :]).then_inc(ug_in, 16)

            def load_x_prep(r, s, first):
                if s < 2:
                    if not first:
                        sp.wait_ge(S_["p_norm"], 4 * r)
                        sp.wait_ge(y_out[s], START + 16 * r - 16)
                        sp.wait_ge(xn_out[s % 2], 32 * r)
                else:
                    sp.wait_ge(xn_out[s % 2], 32 * r + 16)
                    sp.wait_ge(S_["p_norm"], 4 * r + s - 1)
                sp.dma_start(xb[:, s % 2, :], xv[r, s, :, :]).then_inc(xb_in[s % 2], 16)

            def store_x_new(r, s):
                sp.wait_ge(S_["x_new"], 4 * r + s + 1)
                sp.dma_start(xn_dram[r, s, :, :], xb[:, s % 2, :]).then_inc(xn_out[s % 2], 16)

            def load_x_final(n, s, r):
                if r is not None and s < 2:
                    sp.wait_ge(S_["p_norm"], 4 * r + s + 3)
                    sp.wait_ge(xn_out[s % 2], 32 * r + 32)
                elif r is not None:
                    sp.wait_ge(S_["hT2_mm"], 4 * r + s + 1)
                else:
                    sp.wait_ge(y_out[s], START + 16 * n)
                    sp.wait_ge(xn_out[s % 2], 32 * n + 32)
                sp.dma_start(fin[s], xn_dram[n, s, :, :]).then_inc(fin_in[s], 16)

            def store_out(n, s):
                sp.wait_ge(S_["out_ok"], START + 4 * n + s + 1)
                sp.dma_start(ov[n, s, :, :], fin[s]).then_inc(y_out[s], 16)

            def prep(r, m):
                load_ug(r, m)
                load_x_prep(r, 0, False)
                load_x_prep(r, 1, False)
                for s in range(NSUB):
                    store_x_new(r, s)
                    if s < 2:
                        load_x_prep(r, s + 2, False)

            for item in PROLOGUE:
                kind, q = item[0], item[1]
                if kind == "xT" and q < TPB - 1:
                    load_x_attn(q + 1, item[2])
                if kind == "mod" and q < NMOD - 1:
                    load_mod(q + 1)
                if kind == "modT" and q == 4:
                    sp.wait_ge(S_["mod_fix"], 2 * FIXES)
                    sp.dma_start(gb_dram, mrow[:, GB * D:(GB + 1) * D]).then_inc(S_["gb_saved"], 16)
                if kind == "gate":
                    store_ug(q, item[2])
                    if q == TPB - 1 and item[2] == 0:
                        load_ug(0, TPB - 2)
                if kind == "dq" and UNITS[q][1] == 0 and UNITS[q][0] + 1 < len(GROUPS) and UNITS[q][0] >= 1:
                    load_scales(UNITS[q][0] + 1)
                if kind == "sum":
                    load_x_prep(0, 0, True)
                    load_x_prep(0, 1, True)
            for s in range(NSUB):
                store_x_new(0, s)
                if s < 2:
                    load_x_prep(0, s + 2, True)

            def step(n, j, with_a, with_p):
                m, r = n + TPB, n + 1
                if j == 0:
                    if not isinstance(n, int) or n > 0:
                        sp.wait_ge(S_["out_ok"], START + 4 * n)
                    sp.wait_ge(S_["dq_w2"], NU)
                    sp.wait_ge(S_["gb_saved"], 16)
                    bt = n // TPB if isinstance(n, int) else (n_batch[0])
                    sp.dma_start(gbB[:, :], gb_dram[bt:bt + 1, :].broadcast_to([P, D]) if isinstance(bt, int)
                                 else gb_dram[bass.ds(bt, 1), :].broadcast_to([P, D])).then_inc(S_["gb_in"], 16)
                if with_a:
                    for e in range(DC):
                        store_ug(m, e)
                    if j < TPB - 1:
                        for s in range(NSUB):
                            load_x_attn(m + 1, s)
                if with_p:
                    prep(r, m if with_a else None)
                for s in range(NSUB):
                    load_x_final(n, s, r if with_p else None)
                for s in range(NSUB):
                    store_out(n, s)

            n_batch = [None]
            with sp.Fori(0, NB - 1) as bt:
                n_batch[0] = bt
                for j in range(TPB):
                    step(TPB * bt + j, j, True, True)
            for j in range(TPB):
                step(TPB * (NB - 1) + j, j, False, j < TPB - 1)
            for s in range(NSUB):
                sp.wait_ge(y_out[s], START + 16 * NB * TPB)
            sp.wait_ge(S_["gb_saved"], 16)
            for k in range(2):
                sp.wait_ge(xn_out[k], 32 * NB * TPB)
                sp.wait_ge(ug_out[k], 32 * NB * TPB)

        @block.gpsimd
        def _(pool):
            for first in STARTED["pool"]:
                pool.sem_inc(first, START)
            nc.gpsimd.memset(ident[:, :], 0.0).then_inc(S_["const_ok"], 1)
            nc.gpsimd.memset(k_pow[:, :], -0.5).then_inc(S_["const_ok"], 1)
            nc.gpsimd.memset(k_eps[:, 0:1], LN_EPS).then_inc(S_["const_ok"], 1)
            nc.gpsimd.memset(k_eps[:, 1:2], RMS_EPS * SHIFT_UP ** -2).then_inc(S_["const_ok"], 1)
            pool.wait_ge(S_["const_ok"], 4)
            nc.gpsimd.affine_select(out=ident[:, :], in_=ident[:, :], compare_op=ALU.not_equal, fill=1.0,
                                    base=0, pattern=[[-1, P]], channel_multiplier=1).then_inc(S_["ident_ok"], 1)
            pool.wait_ge(S_["ident_ok"], 1)
            nc.gpsimd.tensor_copy(ident16[:, :], ident[:, :]).then_inc(S_["ident_ok"], 1)

            def rstd(mv, rs, s, got, mid, done, idx):
                pool.wait_ge(S_[got], idx + 1)
                nc.gpsimd.tensor_tensor(rs[:, s % 2, 0:1], mv[:, s % 2, 1:2], k_eps[:, 0:1],
                                        ALU.add).then_inc(S_[mid], 1)
                pool.wait_ge(S_[mid], idx + 1)
                nc.gpsimd.tensor_tensor(rs[:, s % 2, 1:2], rs[:, s % 2, 0:1], k_pow[:, :],
                                        ALU.pow).then_inc(S_[done], 1)

            def rstd_a(m, s):
                rstd(mvA, rsA, s, "a_mv", "a_eps", "a_rstd", 4 * m + s)

            def rstd_p(r, s):
                rstd(mvP, rsP, s, "p_mv", "p_eps", "p_rstd", 4 * r + s)

            def final(n):
                for s in range(NSUB):
                    pool.wait_ge(S_["sq_ok"], START + 4 * n + s + 1)
                    nc.gpsimd.tensor_tensor(rms[:, s, 0:1], ssq[:, s:s + 1], k_eps[:, 1:2],
                                            ALU.add).then_inc(S_["rms_a"], 1)
                    pool.wait_ge(S_["rms_a"], 4 * n + s + 1)
                    nc.gpsimd.tensor_tensor(rms[:, s, 1:2], rms[:, s, 0:1], k_pow[:, :],
                                            ALU.pow).then_inc(S_["rms_ok"], 1)

            def dq_low(uu):
                pool.wait_ge(S_["dq_w1"], uu + 1)
                nc.gpsimd.tensor_tensor(dq_dst(uu, 1), raw[:, uu % 2, 0:P * UNITS[uu][2]], dq_dst(uu, 0).bitcast(F32),
                                        ALU.subtract).then_inc(S_["dq_w2"], 1)

            def chunk_h2(n, i):
                q = NCH * n + i
                pool.wait_ge(S_["h1_ok"], q + 1)
                if i:
                    pool.wait_ge(S_["d_mm"], START + (NCH - 1) * n + i)
                else:
                    pool.wait_ge(S_["y_mm"], START + 4 * n)
                nc.gpsimd.tensor_tensor(H2[:, :], S[:, i % 2, :], H1[:, i % 2, :].bitcast(F32),
                                        ALU.subtract).then_inc(S_["h2_ok"], 1)

            for s in range(NSUB):
                rstd_a(0, s)
            for item in PROLOGUE:
                kind, q = item[0], item[1]
                if kind == "norm":
                    rstd_a(q, 2 * item[2])
                    rstd_a(q, 2 * item[2] + 1)
                if kind == "dq":
                    dq_low(q)
                if kind == "yT" and q:
                    rstd_p(0, q - 1)
                if item == ("hT2", 1):
                    rstd_p(0, NSUB - 1)
            for k in range(DC):
                pool.wait_ge(S_["g_hi"], k + 1)
                nc.gpsimd.tensor_tensor(WG2[:, k, :], WG[:, k, :], WG1[:, k, :].bitcast(F32),
                                        ALU.subtract).then_inc(S_["g_lo"], 1)

            def step(n, j, with_a, with_p):
                for i in range(NCH):
                    if with_a and i in (0, 1):
                        rstd_a(n + TPB, 2 * i)
                        rstd_a(n + TPB, 2 * i + 1)
                    chunk_h2(n, i)
                    for s in late(j - 1, with_a) if i == 0 and j else ():
                        add_out(n - 1, s, j - 1, with_a)
                    if with_a and i in (3, 4):
                        for e in (2 * i - 6, 2 * i - 5):
                            h_sum(n + TPB, e)
                    if with_p:
                        for s in {7: (0, 1), 8: (2,), 9: (3,)}.get(i, ()):
                            rstd_p(n + 1, s)
                final(n)
                for s in range(NSUB - len(late(j, with_a))):
                    add_out(n, s, j, with_a)

            def h_sum(m, e):
                pool.wait_ge(S_["h2a_ok"], 4 * (m - TPB) + e + 1)
                if e < 2:
                    pool.wait_ge(ug_out[e], 32 * m)
                    pool.wait_ge(S_["out_ok"], START + 4 * (m - TPB))
                else:
                    pool.wait_ge(ug_out[e % 2], 32 * m + 16)
                nc.gpsimd.tensor_tensor(ugo[:, e % 2, :], h_hi[:, e, :].bitcast(F32),
                                        h_lo[:, e, :].bitcast(F32), ALU.add
                                        ).then_inc(S_["hsum_ok"], 1)

            def add_out(n, s, j, with_a):
                pool.wait_ge(fin_in[s], 16 * n + 16)
                pool.wait_ge(S_["y_used"], START + 4 * n + s + 1)
                nc.gpsimd.tensor_tensor(fin[s], yo(s, j, with_a), fin[s], ALU.add).then_inc(S_["out_ok"], 1)

            with pool.Fori(0, NB - 1) as bt:
                for j in range(TPB):
                    step(TPB * bt + j, j, True, True)
            for j in range(TPB):
                step(TPB * (NB - 1) + j, j, False, j < TPB - 1)

        @block.scalar
        def _(act):
            for first in STARTED["act"]:
                act.sem_inc(first, START)
            def batch_cols(dst, rows, bt, done):
                for i, row in enumerate(rows):
                    src = modT[:, bass.ds(bt, 1), row, :] if not isinstance(bt, int) else modT[:, bt:bt + 1, row, :]
                    ins = nc.scalar.activation(dst[:, i:i + 1, :], src, ACT.Copy)
                ins.then_inc(S_[done], 1)
                act.wait_ge(S_[done], bt + 1)

            def x_evac(m, s, j, n):
                if j == 0 and s == 0:
                    batch_cols(modA, (SA, CA), bt_of(m), "modA_ok")
                act.wait_ge(S_["xT_mm"], 4 * m + s + 1)
                if s == 0 and n is not None:
                    act.wait_ge(S_["x2_ok"], 4 * n + 4)
                if s == 0 and early_tile(m) and m >= 2:
                    act.wait_ge(S_["ug_done"], 4 * m - 4)
                src = xT_banks[s % 2] if early_tile(m) else bank_of(("xT", s))
                for c_ in range(DC):
                    ins = nc.scalar.activation(hT_of(m)[:, c_, P * s:P * (s + 1)], src[:, P * c_:P * (c_ + 1)],
                                               ACT.Identity, bias=modA[:, 0, c_:c_ + 1], scale=modA[:, 1, c_:c_ + 1])
                ins.then_inc(S_["hT_ok"], 1)

            def gate_sig(m, e):
                act.wait_ge(S_["gate_mm"], 4 * m + e + 1)
                if e < 2:
                    if isinstance(m, int):
                        if m:
                            act.wait_ge(S_["ug_done"], 4 * m + e - 1)
                    else:
                        act.wait_ge(y_out[2 + e], START + 16 * (m - TPB))
                        act.wait_ge(S_["hT2_mm"], 4 * (m - TPB) + 4)
                else:
                    act.wait_ge(S_["ug_done"], 4 * m + e - 1)
                nc.scalar.activation(two[:, e % 2, :], bank_of(("gate", e))[:, :], ACT.Sigmoid,
                                     bias=vec[:, 4, e:e + 1]).then_inc(S_["gate_sig"], 1)

            def h_evac(r, s, j_r):
                if j_r == 0 and s == 0:
                    batch_cols(modP, (SB, CB), bt_of(r), "modP_ok")
                act.wait_ge(S_["hT2_mm"], 4 * r + s + 1)
                src = bank_of(("hT2", s))
                for c_ in range(DC):
                    ins = nc.scalar.activation(chan[:, c_, P * s:P * (s + 1)], src[:, P * c_:P * (c_ + 1)],
                                               ACT.Identity, bias=modP[:, 0, c_:c_ + 1], scale=modP[:, 1, c_:c_ + 1])
                ins.then_inc(S_["x_next"], 1)

            def split_x(r, c_, ffn_before):
                if c_ == 0:
                    act.wait_ge(S_["x_next"], 4 * r + 4)
                    if ffn_before:
                        act.wait_ge(S_["u_mm"], NCH * r)
                nc.scalar.activation(X1[:, c_, :], chan[:, c_, :], ACT.Copy).then_inc(S_["x1_ok"], 1)

            def chunk_sig(n, i):
                q = NCH * n + i
                act.wait_ge(S_["g_mm"], q + 1)
                act.wait_ge(S_["h2_ok"], START + (q - 1 if i else q))
                if i == 1:
                    act.wait_ge(S_["sq_ok"], START + 4 * n)
                nc.scalar.activation(S[:, i % 2, :], gps[:, :], ACT.Sigmoid, scale=SHIFT_UP).then_inc(S_["sig_ok"], 1)

            def chunk_h1(n, i):
                q = NCH * n + i
                act.wait_ge(S_["h_ok"], START + q + 1)
                if i == 0:
                    act.wait_ge(S_["y_mm"], START + 4 * n)
                else:
                    act.wait_ge(S_["d_mm"], START + (NCH - 1) * n + i - 1)
                nc.scalar.activation(H1[:, i % 2, :], S[:, i % 2, :], ACT.Copy).then_inc(S_["h1_ok"], 1)

            def final(n):
                act.wait_ge(S_["h2_ok"], START + NCH * n + NCH - 1)
                for s in range(NSUB):
                    act.wait_ge(S_["y_mm"], START + 4 * n + s + 1)
                    if s:
                        act.wait_ge(S_["sq_ok"], START + 4 * n + s)
                    nc.scalar.activation(S[:, 1, :], yps[s][:, :], ACT.Square, scale=float(D) ** -0.5,
                                         accum_out=ssq[:, s:s + 1]).then_inc(S_["sq_ok"], 1)

            cur = {}

            def bt_of(t):
                return t // TPB if isinstance(t, int) else cur["bt"] + 1

            act.wait_ge(S_["cond_in"], 16)
            nc.scalar.activation(csig, crow, ACT.Sigmoid).then_inc(S_["csig_ok"], 1)
            act.wait_ge(S_["cT_mm"], 1)
            nc.scalar.activation(cT[:, :, :], bank[0][:, 0:DC * NB].rearrange("p (c b) -> p c b", b=NB),
                                 ACT.Copy).then_inc(S_["cT_ok"], 1)

            def mod(t):
                i = MODS[t]
                act.wait_ge(S_["mod_mm"], t + 1)
                dst, src = mrow[:, D * i:D * (i + 1)], modps[0:NB, :]
                if i in (SB, CB):
                    dst = dst.rearrange("b (c j w) -> b c w j", j=8, w=WPG)
                    src = src.rearrange("b (c w j) -> b c w j", j=8, w=WPG)
                nc.scalar.activation(dst, src, ACT.Identity,
                                     bias=1.0 if i in (CA, CB) else 0.0).then_inc(S_["mod_row"], 1)

            def mod_T(t):
                act.wait_ge(S_["modt_mm"], MOD_T.index(t) + 1)
                nc.scalar.activation(modT[:, :, MODS[t], :],
                                     modps[:, 0:DC * NB].rearrange("p (c b) -> p b c", b=NB),
                                     ACT.Copy).then_inc(S_["modt_ok"], 1)

            def dq(uu):
                if uu == GROUP_END[DC - 1] and uu < FIRST_UNDER_END:
                    act.wait_ge(S_["gb_saved"], 16)
                if uu == FIRST_UNDER_END:
                    act.wait_ge(S_["ug_done"], 4 * TPB)
                    act.wait_ge(S_["xT_mm"], 4 * TPB)
                act.wait_ge(S_["dq_raw"], uu + 1)
                nc.scalar.activation(dq_dst(uu, 0), raw[:, uu % 2, 0:P * UNITS[uu][2]],
                                     ACT.Copy).then_inc(S_["dq_w1"], 1)

            mod(0)
            mod_T(0)
            mod(1)
            mod_T(1)
            for k in range(DC):
                act.wait_ge(S_["gw_mm"], k + 1)
                nc.scalar.activation(WG[:, k, :], bank[k % 2][:, :], ACT.Copy).then_inc(S_["gw_ok"], 1)
            act.wait_ge(S_["vec_in"], 80)
            nc.scalar.activation(aa[:, :], vec[:, 0, :], ACT.Tanh).then_inc(S_["vec_tanh"], 1)
            act.wait_ge(S_["modt_ok"], 2)
            for item in PROLOGUE:
                kind, q = item[0], item[1]
                if kind == "xT":
                    x_evac(q, item[2], q, None)
                elif kind == "gate":
                    gate_sig(q, item[2])
                elif kind == "dq":
                    dq(q)
                elif kind == "mod":
                    mod(q)
                elif kind == "modT":
                    mod_T(q)
                elif kind == "hT2":
                    if q == 0:
                        act.wait_ge(S_["modt_ok"], len(MOD_T))
                    h_evac(0, q, 0)
            act.wait_ge(S_["dq_w2"], NU)
            for c_ in range(DC):
                split_x(0, c_, False)
            act.wait_ge(S_["gate_mm"], 4 * TPB)
            for k in range(DC):
                nc.scalar.activation(WG1[:, k, :], WG[:, k, :], ACT.Copy).then_inc(S_["g_hi"], 1)

            def load_rows(m, subs):
                for s in subs:
                    nc.scalar.dma_start(rows[:, s, :], xv[m, s, :, :]).then_inc(xa_in[s], 16)

            def split_h(m):
                act.wait_ge(S_["hT_ok"], 4 * m + 4)
                for k in range(DC):
                    nc.scalar.activation(h_hi[:, k, :], chan[:, k, :], ACT.Copy).then_inc(S_["h1a_ok"], 1)

            def step(n, j, with_a, with_p):
                m, r = n + TPB, n + 1
                for i in range(NCH):
                    if with_a and j == 0 and i == 0:
                        act.wait_ge(S_["gate_mm"], 4 * m)
                        load_rows(m, (0, 1))
                    chunk_sig(n, i)
                    if with_a and j == 0 and i == 1:
                        act.wait_ge(S_["out_ok"], START + 4 * n)
                        load_rows(m, (2, 3))
                    chunk_h1(n, i)
                    if with_a:
                        if i in (1, 2):
                            for s in (2 * i - 2, 2 * i - 1):
                                x_evac(m, s, j, n)
                        if i == 2:
                            split_h(m)
                        if i in (3, 4):
                            for e in (2 * i - 6, 2 * i - 5):
                                gate_sig(m, e)
                    if with_p:
                        for s in {8: (0,), 9: (1,), 10: (2, 3)}.get(i, ()):
                            h_evac(r, s, (j + 1) % TPB)
                if with_p:
                    for c_ in range(DC):
                        split_x(r, c_, True)
                final(n)

            with act.Fori(0, NB - 1) as bt:
                cur["bt"] = bt
                for j in range(TPB):
                    step(TPB * bt + j, j, True, True)
            for j in range(TPB):
                step(TPB * (NB - 1) + j, j, False, j < TPB - 1)

        @block.vector
        def _(dve):
            for first in STARTED["dve"]:
                dve.sem_inc(first, START)

            def norm_rows(m, h):
                s0 = 2 * h
                k = 4 * m + s0
                dve.wait_ge(S_["a_norm"], k)
                dve.wait_ge(S_["a_mv"], k)
                dve.wait_ge(xa_in[s0], 16 * m + 16)
                nc.vector.bn_stats(stat[:, 0, :], rows[:, s0, :]).then_inc(S_["a_stat"], 1)
                dve.wait_ge(xa_in[s0 + 1], 16 * m + 16)
                dve.wait_ge(S_["a_stat"], k + 1)
                nc.vector.bn_stats(stat[:, 1, :], rows[:, s0 + 1, :]).then_inc(S_["a_stat"], 1)
                nc.vector.bn_aggr(mvA[:, 0, :], stat[:, 0, :]).then_inc(S_["a_mv"], 1)
                dve.wait_ge(S_["a_stat"], k + 2)
                norm_a(m, s0)
                nc.vector.bn_aggr(mvA[:, 1, :], stat[:, 1, :]).then_inc(S_["a_mv"], 1)
                norm_a(m, s0 + 1)

            def norm_a(m, s):
                k = 4 * m + s
                dve.wait_ge(S_["a_rstd"], k + 1)
                nc.vector.tensor_scalar(rows[:, s, :], rows[:, s, :], mvA[:, s % 2, 0:1], rsA[:, s % 2, 1:2],
                                        ALU.subtract, ALU.mult).then_inc(S_["a_norm"], 1)

            def gated(m, e, j):
                k = 4 * m + e
                dve.wait_ge(S_["gate_sig"], k + 1)
                if early_tile(m):
                    if k >= 2:
                        dve.wait_ge(ug_out[e % 2], 32 * m + 16 * (e // 2))
                    h_ = hT_of(m)[:, e, :]
                else:
                    dve.wait_ge(S_["hsum_ok"], k - 4 * TPB + 1)
                    h_ = ugo[:, e % 2, :]
                nc.vector.scalar_tensor_tensor(out=ugo[:, e % 2, :], in0=h_, scalar=1.0,
                                               in1=two[:, e % 2, :], op0=ALU.mult, op1=ALU.mult,
                                               accum_out=usum[:, e, j:j + 1]).then_inc(S_["ug_done"], 1)

            def u_total(bt, m):
                dve.wait_ge(S_["ug_done"], 4 * m + 4)
                nc.vector.reduce_sum(umean[:, :], usum[:, :, :], mybir.AxisListType.X).then_inc(S_["um_done"], 1)

            def new_coef(bt):
                dve.wait_ge(S_["lr_in"], 16 * (1 + DC))
                dve.wait_ge(S_["lr_mm"], bt + 1)
                by_rank = bank_of(("lr", 0))[:, 0:RANK].unsqueeze(1).broadcast_to([P, DC, RANK])
                nc.vector.tensor_tensor(lrp[:, :, :], by_rank, lrv[:, :, :], ALU.mult).then_inc(S_["lr_prod"], 1)
                dve.wait_ge(S_["lr_prod"], bt + 1)
                nc.vector.reduce_sum(dlr[:, :], lrp[:, :, :], mybir.AxisListType.X).then_inc(S_["lr_sum"], 1)
                dve.wait_ge(S_["lr_sum"], bt + 1)
                nc.vector.scalar_tensor_tensor(out=deff[:, :], in0=dlr[:, :],
                                               scalar=1.0 / (T * max(1.0, float(RANK))), in1=vec[:, 3, :],
                                               op0=ALU.mult, op1=ALU.add).then_inc(S_["d_eff"], 1)
                ga = modT[:, bt, GA, :] if isinstance(bt, int) else \
                    modT[:, bass.ds(bt, 1), GA, :].rearrange("p o c -> p (o c)")
                nc.vector.tensor_tensor(coef[:, 0, :], bc_[:, :], ga, ALU.mult).then_inc(S_["d_tmp"], 1)
                dve.wait_ge(S_["d_eff"], bt + 1)
                nc.vector.tensor_tensor(coef[:, 1, :], deff[:, :], ga, ALU.mult).then_inc(S_["coef_ok"], 1)

            def scan(r, e, j):
                k = 4 * r + e
                if e == 0:
                    dve.wait_ge(ug_in, 16 * r + 16)
                    bt = bt_of(r)
                    dve.wait_ge(S_["coef_ok"], bt + 1)
                    dve.wait_ge(S_["d_tmp"], bt + 1)
                if e < 2:
                    if not (isinstance(r, int) and r == 0):
                        dve.wait_ge(S_["hT2_mm"], 4 * r)
                        dve.wait_ge(y_out[2 + e], START + 16 * (r - 1))
                    dve.wait_ge(S_["ug_done"], scan_floor(r, e))
                else:
                    dve.wait_ge(S_["yT_ok"], k - 1)
                st = two[:, e % 2, :]
                if j == 0:
                    bt = bt_of(r)
                    nc.vector.tensor_tensor(st[:, 0:1], chan[:, e, 0:1], f0[:, e:e + 1],
                                            ALU.mult).then_inc(S_["p_first"], 1)
                    dve.wait_ge(S_["p_first"], 4 * bt + e + 1)
                    nc.vector.tensor_tensor_scan(st[:, 1:TOK], aa[:, e:e + 1].broadcast_to([P, TOK - 1]),
                                                 chan[:, e, 1:TOK], st[:, 0:1], ALU.mult, ALU.add
                                                 ).then_inc(S_["p_scan"], 1)
                else:
                    dve.wait_ge(S_["carry_ok"], 4 * (r - 1) + e + 1)
                    nc.vector.tensor_tensor_scan(st, aa[:, e:e + 1].broadcast_to([P, TOK]), chan[:, e, :],
                                                 carry[:, e:e + 1], ALU.mult, ALU.add).then_inc(S_["p_scan"], 1)
                dve.wait_ge(S_["p_scan"], k + 1)
                nc.vector.tensor_copy(carry[:, e:e + 1], st[:, TOK - 1:TOK]).then_inc(S_["carry_ok"], 1)
                nc.vector.tensor_scalar(chan[:, e, :], chan[:, e, :], coef[:, 1, e:e + 1], None,
                                        ALU.mult).then_inc(S_["p_mul"], 1)
                dve.wait_ge(S_["p_mul"], k + 1)
                nc.vector.scalar_tensor_tensor(out=chan[:, e, :], in0=st, scalar=coef[:, 0, e:e + 1],
                                               in1=chan[:, e, :], op0=ALU.mult, op1=ALU.add
                                               ).then_inc(S_["yT_ok"], 1)

            def scan_floor(r, e):
                if isinstance(r, int):
                    return 4 * min(r + TPB, NB * TPB) if r else 4 * TPB
                return 4 * (r + TPB)

            def add_x(r, s, after=None):
                k = 4 * r + s
                dve.wait_ge(S_["yT_mm"], k + 1)
                dve.wait_ge(xb_in[s % 2], 32 * r + 16 * (s // 2) + 16)
                if after is not None:
                    dve.wait_ge(S_["p_stat"], 4 * r + after + 1)
                nc.vector.tensor_tensor(xb[:, s % 2, :], bank_of(("yT", s))[:, :], xb[:, s % 2, :],
                                        ALU.add).then_inc(S_["x_new"], 1)
                if after is not None:
                    aggr_p(r, after)
                dve.wait_ge(S_["x_new"], k + 1)
                if not (isinstance(r, int) and k < 2):
                    dve.wait_ge(S_["p_mv"], k - 1)
                    dve.wait_ge(S_["p_norm"], k - 1)
                nc.vector.bn_stats(stat[:, 2 + s % 2, :], xb[:, s % 2, :]).then_inc(S_["p_stat"], 1)

            def aggr_p(r, s):
                nc.vector.bn_aggr(mvP[:, s % 2, :], stat[:, 2 + s % 2, :]).then_inc(S_["p_mv"], 1)

            def norm_p(r, s, after=None):
                k = 4 * r + s
                dve.wait_ge(S_["p_rstd"], k + 1)
                if s < 2:
                    dve.wait_ge(S_["yT_ok"], 4 * r + 4)
                else:
                    dve.wait_ge(S_["hT2_mm"], k - 1)
                if after is not None:
                    dve.wait_ge(S_["p_stat"], 4 * r + after + 1)
                dst = two[:, s % 2, :].rearrange("p (g j w) -> p g w j", j=8, w=WPG)
                src = xb[:, s % 2, :].rearrange("p (g w j) -> p g w j", j=8, w=WPG)
                nc.vector.tensor_scalar(dst, src, mvP[:, s % 2, 0:1], rsP[:, s % 2, 1:2],
                                        ALU.subtract, ALU.mult).then_inc(S_["p_norm"], 1)
                if after is not None:
                    aggr_p(r, after)

            def split_x(r, c_):
                dve.wait_ge(S_["x1_ok"], 4 * r + c_ + 1)
                nc.vector.tensor_tensor(X2[:, c_, :], chan[:, c_, :], X1[:, c_, :].bitcast(F32),
                                        ALU.subtract).then_inc(S_["x2_ok"], 1)

            def chunk_h(n, i, between=None):
                q = NCH * n + i
                s_ = S[:, i % 2, :]
                dve.wait_ge(S_["sig_ok"], q + 1)
                nc.vector.scalar_tensor_tensor(out=s_, in0=gps[:, :], scalar=SHIFT_UP, in1=s_,
                                               op0=ALU.mult, op1=ALU.mult).then_inc(S_["gs_ok"], 1)
                if between is not None:
                    between()
                dve.wait_ge(S_["u_mm"], q + 1)
                dve.wait_ge(S_["gs_ok"], START + q + 1)
                nc.vector.scalar_tensor_tensor(out=s_, in0=ups[:, :], scalar=SHIFT_UP, in1=s_,
                                               op0=ALU.mult, op1=ALU.mult).then_inc(S_["h_ok"], 1)

            def split_h(m):
                for k in range(DC):
                    dve.wait_ge(S_["h1a_ok"], 4 * (m - TPB) + k + 1)
                    nc.vector.tensor_tensor(h_lo[:, k, :], chan[:, k, :], h_hi[:, k, :].bitcast(F32),
                                            ALU.subtract).then_inc(S_["h2a_ok"], 1)

            def final(n, bt, j, with_a, subs):
                for s in subs:
                    if s == 0:
                        dve.wait_ge(S_["gb_in"], 16 * bt + 16)
                        dve.wait_ge(S_["out_ok"], START + 4 * n)
                    if s < 2:
                        done = min(n + 1 + TPB, NB * TPB) if isinstance(n, int) else n + 1 + TPB
                        dve.wait_ge(ug_out[s], 32 * done)
                    elif not wide(j, with_a):
                        dve.wait_ge(S_["out_ok"], START + 4 * n + s - 1)
                    elif with_a:
                        dve.wait_ge(S_["gate_mm"], 4 * (n + 1 + TPB))
                    dve.wait_ge(S_["rms_ok"], 4 * n + s + 1)
                    nc.vector.scalar_tensor_tensor(out=yo(s, j, with_a), in0=yps[s][:, :], scalar=rms[:, s, 1:2],
                                                   in1=gbB[:, :], op0=ALU.mult, op1=ALU.mult
                                                   ).then_inc(S_["y_used"], 1)

            cur = {}

            def bt_of(t):
                return t // TPB if isinstance(t, int) else cur["bt_" + str(cur["which"])]

            dve.wait_ge(S_["csig_ok"], 1)
            nc.vector.tensor_tensor(csig, csig, crow, ALU.mult).then_inc(S_["silu_ok"], 1)
            norm_rows(0, 0)
            norm_rows(0, 1)

            dve.wait_ge(S_["vec_tanh"], 1)
            nc.vector.tensor_scalar(f0[:, :], aa[:, :], 1e-6, None, ALU.max).then_inc(S_["vec_fix"], 1)
            nc.vector.tensor_tensor(bc_[:, :], vec[:, 1, :], vec[:, 2, :], ALU.mult).then_inc(S_["vec_fix"], 1)
            dve.wait_ge(S_["vec_fix"], 2)
            nc.vector.reciprocal(f0[:, :], f0[:, :]).then_inc(S_["vec_fix"], 1)
            dve.wait_ge(S_["vec_fix"], 3)
            nc.vector.tensor_tensor(f0[:, :], f0[:, :], aa[:, :], ALU.mult).then_inc(S_["vec_fix"], 1)
            dve.wait_ge(S_["vec_fix"], 4)

            def mod_fix(k, row):
                g_ = mrow[:, D * row:D * (row + 1)]
                dve.wait_ge(S_["mod_row"], MODS.index(row) + 1)
                nc.vector.tensor_scalar(mtmp[:, :], g_, 0.0, 2.0, ALU.is_ge, ALU.mult).then_inc(S_["mod_fix"], 1)
                dve.wait_ge(S_["mod_fix"], FIXES * k + 1)
                nc.vector.tensor_scalar(mtmp[:, :], mtmp[:, :], 1.0, None, ALU.subtract).then_inc(S_["mod_fix"], 1)
                nc.vector.scalar_tensor_tensor(out=g_, in0=g_, scalar=-1.0, in1=g_,
                                               op0=ALU.mult, op1=ALU.max).then_inc(S_["mod_fix"], 1)
                dve.wait_ge(S_["mod_fix"], FIXES * k + 3)
                nc.vector.scalar_tensor_tensor(out=g_, in0=g_, scalar=0.25, in1=mtmp[:, :],
                                               op0=ALU.max, op1=ALU.mult).then_inc(S_["mod_fix"], 1)
                dve.wait_ge(S_["mod_fix"], FIXES * (k + 1))

            def dq_unpack(gi):
                kind, c0, n_ = GROUPS[gi]
                if gi == 0:
                    dve.wait_ge(S_["gpk_in"], 16 * 8)
                else:
                    if gi == DC:
                        dve.wait_ge(S_["dpk_in"], 16)
                    dve.wait_ge(S_["dq_mm"], GROUP_END[gi - 1])
                if kind == "gu":
                    words = gpk[:, :, WPG * c0:WPG * (c0 + 1)]
                    out_ = nib[:, :].rearrange("p (o j w) -> p o j w", j=8, w=WPG)
                    size = 2 * HID
                else:
                    words = dpk[:, :, WPG * c0:WPG * (c0 + n_)].rearrange("p h (c w) -> p h c w", w=WPG)
                    size = DC * n_ * P
                    out_ = nib[:, 0:size].rearrange("p (h c j w) -> p h c j w", c=n_, j=8, w=WPG)
                for j in range(8):
                    ins = nc.vector.tensor_scalar(out_[:, :, j, :] if kind == "gu" else out_[:, :, :, j, :], words,
                                                  28 - 4 * j, 3, ALU.logical_shift_left, ALU.arith_shift_right)
                ins.then_inc(S_["dq_top"], 1)
                dve.wait_ge(S_["dq_top"], gi + 1)
                nc.vector.tensor_scalar(nib[:, 0:size], nib[:, 0:size], -0x72000000, None,
                                        ALU.bitwise_and).then_inc(S_["dq_nib"], 1)

            def dq(uu):
                gi, b0, nb_, kind, ch, col = UNITS[uu]
                if uu >= 2:
                    dve.wait_ge(S_["dq_w2"], uu - 1)
                at = col if kind == "gu" else D * (ch - GROUPS[gi][1])
                dve.wait_ge(scl_in[gi % 2], 16 * (gi // 2) + 16)
                dve.wait_ge(S_["dq_mm"], uu + 1)
                scale, dst = scl[:, gi % 2, at:at + P * nb_], raw[:, uu % 2, 0:P * nb_]
                val = dq_banks[uu % NDQ][:, :].bitcast(F16)[:, 0:P * nb_]
                if kind == "gu":
                    scale = scale.rearrange("p (c w j) -> p c j w", w=WPG, j=8)
                    val = val.rearrange("p (c j w) -> p c j w", w=WPG, j=8)
                    dst = dst.rearrange("p (c j w) -> p c j w", w=WPG, j=8)
                nc.vector.tensor_tensor(dst, val, scale, ALU.mult).then_inc(S_["dq_raw"], 1)

            cur["which"] = "p"
            for item in PROLOGUE:
                kind, q = item[0], item[1]
                if kind == "norm":
                    norm_rows(q, item[2])
                elif kind == "gate":
                    gated(q, item[2], q)
                elif kind == "unpack":
                    dq_unpack(q)
                elif kind == "dq":
                    dq(q)
                elif kind == "fix":
                    mod_fix((GA, GB).index(MODS[q]), MODS[q])
                elif kind == "sum":
                    u_total(0, TPB - 1)
                elif kind == "deff":
                    dve.wait_ge(S_["modt_ok"], len(MOD_T))
                    new_coef(0)
                elif kind == "scan":
                    scan(0, q, 0)
                elif kind == "yT":
                    if q == 2:
                        norm_p(0, 0, after=1)
                    if q == 3:
                        norm_p(0, 1, after=2)
                    add_x(0, q, after={1: 0}.get(q))
                elif item == ("hT2", 1):
                    norm_p(0, 2, after=3)
                    norm_p(0, 3)
            for c_ in range(DC):
                split_x(0, c_)

            def step(n, j, bt, with_a, with_p):
                m, r = n + TPB, n + 1
                cur["bt_p"] = bt + 1 if j == TPB - 1 else bt
                for i in range(NCH):
                    if i == 0 and j:
                        rest = late(j - 1, with_a)
                        chunk_h(n, i, between=lambda: final(n - 1, bt, j - 1, with_a, rest[:1]))
                        final(n - 1, bt, j - 1, with_a, rest[1:])
                    else:
                        chunk_h(n, i)
                    if with_a:
                        if i in (0, 1):
                            norm_rows(m, i)
                        if i == 2:
                            split_h(m)
                        if i in (3, 4):
                            for e in (2 * i - 6, 2 * i - 5):
                                gated(m, e, j)
                        if i == 4 and j == TPB - 1:
                            u_total(bt + 1, m)
                        if i == 5 and j == TPB - 1:
                            new_coef(bt + 1)
                    if with_p:
                        turns = {5: (0,), 6: (1, 2, 3)} if j == TPB - 1 else {5: (0, 1), 6: (2, 3)}
                        for e in turns.get(i, ()):
                            scan(r, e, (j + 1) % TPB)
                        if i == 7:
                            add_x(r, 0)
                            add_x(r, 1, after=0)
                            norm_p(r, 0, after=1)
                        if i == 8:
                            add_x(r, 2)
                            norm_p(r, 1, after=2)
                        if i == 9:
                            add_x(r, 3)
                            norm_p(r, 2, after=3)
                            norm_p(r, 3)
                if with_p:
                    for c_ in range(DC):
                        split_x(r, c_)
                final(n, bt, j, with_a, range(NSUB - len(late(j, with_a))))

            with dve.Fori(0, NB - 1) as bt:
                for j in range(TPB):
                    step(TPB * bt + j, j, bt, True, True)
            for j in range(TPB):
                step(TPB * (NB - 1) + j, j, NB - 1, False, j < TPB - 1)

        @block.tensor
        def _(pe):
            for first in STARTED["pe"]:
                pe.sem_inc(first, START)

            def attn_T(bk, m, s):
                dst = bk.take(pe, ("xT", s), m=m)
                pe.wait_ge(S_["a_norm"], 4 * m + s + 1)
                for c_ in range(DC):
                    ins = nc.tensor.transpose(dst[:, P * c_:P * (c_ + 1)], rows[:, s, P * c_:P * (c_ + 1)], ident[:, :])
                ins.then_inc(S_["xT_mm"], 1)

            def gate(bk, m, e):
                dst = bk.take(pe, ("gate", e), m=m)
                if early_tile(m):
                    pe.wait_ge(S_["hT_ok"], 4 * m + 4)
                    for k in range(DC):
                        ins = nc.tensor.matmul(dst[:, :], WG[:, k, P * e:P * (e + 1)], hT_of(m)[:, k, :],
                                               start=(k == 0), stop=(k == DC - 1))
                else:
                    if e == 0:
                        pe.wait_ge(S_["g_lo"], DC)
                    for k in range(DC):
                        if e == 0:
                            pe.wait_ge(S_["h1a_ok"], 4 * (m - TPB) + k + 1)
                        for w in (WG1, WG2):
                            nc.tensor.matmul(dst[:, :], w[:, k, P * e:P * (e + 1)], h_hi[:, k, :],
                                             start=(k == 0 and w is WG1), stop=False)
                    for k in range(DC):
                        if e == 0:
                            pe.wait_ge(S_["h2a_ok"], 4 * (m - TPB) + k + 1)
                        ins = nc.tensor.matmul(dst[:, :], WG1[:, k, P * e:P * (e + 1)], h_lo[:, k, :],
                                               start=False, stop=(k == DC - 1))
                ins.then_inc(S_["gate_mm"], 1)

            def low_rank(bk, bt):
                dst = bk.take(pe, ("lr", 0), bt=bt)
                pe.wait_ge(S_["um_done"], bt + 1)
                for k in range(DC):
                    ins = nc.tensor.matmul(dst[:, 0:RANK], umean[:, k:k + 1].broadcast_to([P, P]), lru[:, k, :],
                                           start=(k == 0), stop=(k == DC - 1))
                ins.then_inc(S_["lr_mm"], 1)

            def y_T(bk, r, s):
                dst = bk.take(pe, ("yT", s), r=r)
                pe.wait_ge(S_["yT_ok"], 4 * r + 4)
                for e in range(DC):
                    ins = nc.tensor.transpose(dst[:, P * e:P * (e + 1)], chan[:, e, P * s:P * (s + 1)], ident[:, :])
                ins.then_inc(S_["yT_mm"], 1)

            def h_T(bk, r, s):
                dst = bk.take(pe, ("hT2", s), r=r)
                pe.wait_ge(S_["p_norm"], 4 * r + s + 1)
                for c_ in range(DC):
                    ins = nc.tensor.transpose(dst[:, P * c_:P * (c_ + 1)], two[:, s % 2, P * c_:P * (c_ + 1)], ident[:, :])
                ins.then_inc(S_["hT2_mm"], 1)

            def piece(bk, p, n, bt):
                kind, s = p
                if kind == "xT":
                    attn_T(bk, n + TPB, s)
                elif kind == "gate":
                    gate(bk, n + TPB, s)
                elif kind == "lr":
                    low_rank(bk, bt + 1)
                elif kind == "yT":
                    y_T(bk, n + 1, s)
                else:
                    h_T(bk, n + 1, s)

            def project(dst, col, n, first, done):
                for k in range(DC):
                    if first:
                        pe.wait_ge(S_["x1_ok"], 4 * n + k + 1)
                    for w in (W1, W2):
                        nc.tensor.matmul(dst[:, :], w[:, k, col:col + P], X1[:, k, :],
                                         start=(k == 0 and w is W1), stop=False)
                for k in range(DC):
                    if first:
                        pe.wait_ge(S_["x2_ok"], 4 * n + k + 1)
                    ins = nc.tensor.matmul(dst[:, :], W1[:, k, col:col + P], X2[:, k, :],
                                           start=False, stop=(k == DC - 1))
                ins.then_inc(S_[done], 1)

            def down(n, i):
                q = NCH * n + i
                pe.wait_ge(S_["h1_ok"], q + 1)
                if i == 0:
                    pe.wait_ge(S_["y_used"], START + 4 * n)
                for s in range(NSUB):
                    for v in (V1, V2):
                        nc.tensor.matmul(yps[s][:, :], H1[:, i % 2, P * s:P * (s + 1)], v[:, i, :],
                                         start=(i == 0 and v is V1), stop=False)
                pe.wait_ge(S_["h2_ok"], START + q + 1)
                for s in range(NSUB):
                    ins = nc.tensor.matmul(yps[s][:, :], H2[:, P * s:P * (s + 1)], V1[:, i, :],
                                           start=False, stop=(i == NCH - 1))
                    if i == NCH - 1:
                        ins.then_inc(S_["y_mm"], 1)
                if i < NCH - 1:
                    ins.then_inc(S_["d_mm"], 1)

            pe.wait_ge(S_["ident_ok"], 2)
            pe.wait_ge(S_["silu_ok"], 1)
            for k in range(DC):
                ins = nc.tensor.transpose(bank[0][:, NB * k:NB * (k + 1)], csig[:, P * k:P * (k + 1)],
                                          ident[0:NB, 0:NB])
            ins.then_inc(S_["cT_mm"], 1)

            def mod(t):
                if t >= 1:
                    pe.wait_ge(S_["mod_row"], t)
                prior = [x for x in MOD_T if x < t]
                if prior:
                    pe.wait_ge(S_["modt_ok"], MOD_T.index(prior[-1]) + 1)
                pe.wait_ge(wm_in[t % 2], 16 * (t // 2) + 16)
                for k in range(DC):
                    ins = nc.tensor.matmul(modps[0:NB, :], cT[:, k, :], wm[:, t % 2, k, :],
                                           start=(k == 0), stop=(k == DC - 1))
                ins.then_inc(S_["mod_mm"], 1)

            def mod_T(t):
                i = MODS[t]
                pe.wait_ge(S_["mod_row"], t + 1)
                if i == GA:
                    pe.wait_ge(S_["mod_fix"], FIXES)
                for c_ in range(DC):
                    ins = nc.tensor.transpose(modps[:, NB * c_:NB * (c_ + 1)],
                                              mrow[:, D * i + P * c_:D * i + P * (c_ + 1)], ident[0:NB, 0:NB])
                ins.then_inc(S_["modt_mm"], 1)

            pe.wait_ge(S_["cT_ok"], 1)
            mod(0)
            mod_T(0)
            mod(1)
            mod_T(1)
            pe.wait_ge(S_["gw_in"], 16)
            for k in range(DC):
                if k >= 2:
                    pe.wait_ge(S_["gw_ok"], k - 1)
                for e in range(DC):
                    ins = nc.tensor.transpose(bank[k % 2][:, P * e:P * (e + 1)], gwr[:, e, P * k:P * (k + 1)],
                                              ident[:, :])
                ins.then_inc(S_["gw_mm"], 1)
            pe.wait_ge(S_["gw_ok"], DC)

            def dq(uu):
                gi, b0, nb_, kind, ch, col = UNITS[uu]
                if uu >= NDQ:
                    pe.wait_ge(S_["dq_raw"], uu - NDQ + 1)
                pe.wait_ge(S_["dq_nib"], gi + 1)
                dst = dq_banks[uu % NDQ][:, :].bitcast(F16)
                for i, blk in enumerate(dq_blocks(uu)):
                    ins = nc.tensor.transpose(dst[:, P * i:P * (i + 1)], blk, ident16[:, :])
                ins.then_inc(S_["dq_mm"], 1)

            bk, bk_xT = Banks(), Banks(xT_banks)
            for item in PROLOGUE:
                kind, q = item[0], item[1]
                if kind == "xT":
                    attn_T(bk_xT, q, item[2])
                elif kind == "gate":
                    gate(bk, q, item[2])
                elif kind == "dq":
                    dq(q)
                elif kind == "mod":
                    mod(q)
                elif kind == "modT":
                    mod_T(q)
                elif kind == "deff":
                    pe.wait_ge(S_["lr_in"], 16 * (1 + DC))
                    low_rank(bk, 0)
                elif kind == "yT":
                    y_T(bk, 0, q)
                elif kind == "hT2":
                    h_T(bk, 0, q)
            pe.wait_ge(S_["dq_w2"], NU)

            SLOT = {1: [("xT", 0), ("xT", 1)], 2: [("xT", 2), ("xT", 3)], 3: [("gate", 0), ("gate", 1)],
                    4: [("gate", 2), ("gate", 3)], 5: [("lr", 0)],
                    7: [("yT", 0), ("yT", 1)], 8: [("yT", 2), ("hT2", 0)], 9: [("yT", 3), ("hT2", 1)],
                    10: [("hT2", 2), ("hT2", 3)]}

            def wanted(p, j, with_a, with_p):
                kind = p[0]
                if kind in ("xT", "gate"):
                    return with_a
                if kind == "lr":
                    return with_a and j == TPB - 1
                return with_p

            def step(bk, n, j, bt, with_a, with_p):
                for i in range(NCH):
                    q = NCH * n + i
                    pe.wait_ge(S_["gs_ok"], START + q)
                    project(gps, P * i, n, i == 0, "g_mm")
                    pe.wait_ge(S_["h_ok"], START + q)
                    project(ups, HID + P * i, n, i == 0, "u_mm")
                    ps = [p for p in SLOT.get(i, []) if wanted(p, j, with_a, with_p)]
                    before = 2 if i == NCH - 1 else 1
                    for p in ps[:before]:
                        piece(bk, p, n, bt)
                    if i:
                        down(n, i - 1)
                    for p in ps[before:]:
                        piece(bk, p, n, bt)
                down(n, NCH - 1)

            with pe.Fori(0, NB - 1) as bt:
                bk.hist = [(("hT2", 2), None, TPB * bt, None), (("hT2", 3), None, TPB * bt, None)]
                for j in range(TPB):
                    step(bk, TPB * bt + j, j, bt, True, True)
            bk = Banks()
            bk.hist = [(("hT2", 2), None, TPB * (NB - 1), None), (("hT2", 3), None, TPB * (NB - 1), None)]
            for j in range(TPB):
                step(bk, TPB * (NB - 1) + j, j, NB - 1, False, j < TPB - 1)


_INS = ['L0_attn_u', 'L0_attn_a', 'L0_attn_b', 'L0_attn_c', 'L0_attn_d', 'L0_attn_gate_w', 'L0_attn_gate_b',
        'L0_attn_d_lr_u', 'L0_attn_d_lr_v', 'L0_ffn_gate_up_packed', 'L0_ffn_gate_up_scales',
        'L0_ffn_down_packed', 'L0_ffn_down_scales', 'L0_c', 'L0_wmod']


def kernel(**inputs):
    import numpy as _np
    import concourse.bacc as _bacc
    from concourse import mybir as _mybir
    from concourse.bass_utils import run_bass_kernel_spmd as _run

    nc = _bacc.Bacc("TRN2", target_bir_lowering=False, num_devices=1)
    arrays, args = {}, []
    for name in _INS:
        a = _np.ascontiguousarray(inputs[name])
        arrays[f"in_{name}_dram"] = a
        args.append(nc.dram_tensor(f"in_{name}_dram", a.shape, _mybir.dt.from_np(a.dtype), kind="ExternalInput").ap())
    shape = tuple(inputs['L0_attn_u'].shape)
    args.append(nc.dram_tensor("out_0_dram", shape, _mybir.dt.from_np(_np.dtype('float32')), kind="ExternalOutput").ap())
    adaln_block_kernel(nc, *args)
    r = _run(nc, [arrays], core_ids=[0])
    return r.results[0]["out_0_dram"]
```
